# Optimizing a Trainium2 kernel written in Bass

```python
import numpy as np
import jax
import jax.numpy as jnp

def _softmax(x, axis=-1):
    return jax.nn.softmax(x, axis=axis)

def _gelu(x):
    return jax.nn.gelu(x, approximate=True)

def _silu(x):
    return jax.nn.silu(x)

def _sigmoid(x):
    return jax.nn.sigmoid(x)

def _layernorm(x, axis=-1, eps=1e-05):
    m = jnp.mean(x, axis=axis, keepdims=True)
    v = jnp.var(x, axis=axis, keepdims=True)
    return (x - m) / jnp.sqrt(v + eps)

def _scatter_add(tgt, idx, src, axis=0):
    return tgt.at[idx].add(src)

def _segment_sum(src, seg, n):
    return jax.ops.segment_sum(src, seg, n)
kernel_name = 'mk_seq_preln_d1_jaxref_r8_80a1b8'

def setup_inputs(seed: int=0):
    np.random.seed(seed)
    _w = jnp.asarray

    def _L0_attn_setup():
        import jax, jax.numpy as jnp
        import numpy as np
        HEAD_NUM = 16
        key = jax.random.key(seed)
        ks = jax.random.split(key, 9)
        B, S, D = (4, 256, 128)

        def xavier(k, shape):
            limit = jnp.sqrt(6.0 / (shape[0] + shape[1]))
            return jax.random.uniform(k, shape, jnp.float32, -limit, limit)
        return {'x': jax.random.normal(ks[0], (B, S, D), jnp.float32), 'Wq': xavier(ks[1], (D, D)), 'bq': jnp.zeros((D,), jnp.float32), 'Wk': xavier(ks[2], (D, D)), 'bk': jnp.zeros((D,), jnp.float32), 'Wv': xavier(ks[3], (D, D)), 'bv': jnp.zeros((D,), jnp.float32), 'Wo': xavier(ks[4], (D, D)), 'bo': jnp.zeros((D,), jnp.float32)}
    _L0_attn_in = _L0_attn_setup()

    def _L0_ffn_setup():
        import jax, jax.numpy as jnp
        import numpy as np
        B, S, D, F, E = (2, 256, 128, 512, 8)
        LN_EPS = 1e-05

        def _layer_norm(x, gamma, beta):
            mu = jnp.mean(x, axis=-1, keepdims=True)
            var = jnp.mean(jnp.square(x - mu), axis=-1, keepdims=True)
            return (x - mu) * jax.lax.rsqrt(var + LN_EPS) * gamma + beta
        key = jax.random.key(seed)
        ks = jax.random.split(key, 8)

        def xavier(k, shape):
            fan_in, fan_out = (shape[-1], shape[-2])
            a = jnp.sqrt(6.0 / (fan_in + fan_out))
            return jax.random.uniform(k, shape, jnp.float32, -a, a)
        return {'tgt': jax.random.normal(ks[0], (B, S, D), jnp.float32), 'Wr': xavier(ks[1], (E, D)), 'br': jnp.zeros((E,), jnp.float32), 'W1': xavier(ks[2], (E, F, D)), 'b1': jnp.zeros((E, F), jnp.float32), 'W2': xavier(ks[3], (E, D, F)), 'b2': jnp.zeros((E, D), jnp.float32), 'gamma': jnp.ones((D,), jnp.float32), 'beta': jnp.zeros((D,), jnp.float32)}
    _L0_ffn_in = _L0_ffn_setup()
    _d = {'L0_attn_x': _L0_attn_in['x'], 'L0_attn_Wq': _L0_attn_in['Wq'], 'L0_attn_bq': _L0_attn_in['bq'], 'L0_attn_Wk': _L0_attn_in['Wk'], 'L0_attn_bk': _L0_attn_in['bk'], 'L0_attn_Wv': _L0_attn_in['Wv'], 'L0_attn_bv': _L0_attn_in['bv'], 'L0_attn_Wo': _L0_attn_in['Wo'], 'L0_attn_bo': _L0_attn_in['bo'], 'L0_ffn_Wr': _L0_ffn_in['Wr'], 'L0_ffn_br': _L0_ffn_in['br'], 'L0_ffn_W1': _L0_ffn_in['W1'], 'L0_ffn_b1': _L0_ffn_in['b1'], 'L0_ffn_W2': _L0_ffn_in['W2'], 'L0_ffn_b2': _L0_ffn_in['b2'], 'L0_ffn_gamma': _L0_ffn_in['gamma'], 'L0_ffn_beta': _L0_ffn_in['beta']}
    _x0 = _d['L0_attn_x']
    _d['L0_attn_x'] = jax.random.normal(jax.random.fold_in(jax.random.key(seed), 1), (8, 512, 128), dtype=_x0.dtype)
    del _x0
    return _d

def reference(L0_attn_x, L0_attn_Wq, L0_attn_bq, L0_attn_Wk, L0_attn_bk, L0_attn_Wv, L0_attn_bv, L0_attn_Wo, L0_attn_bo, L0_ffn_Wr, L0_ffn_br, L0_ffn_W1, L0_ffn_b1, L0_ffn_W2, L0_ffn_b2, L0_ffn_gamma, L0_ffn_beta):

    def _L0_attn_ref(x, Wq, bq, Wk, bk, Wv, bv, Wo, bo):
        import jax, jax.numpy as jnp
        import numpy as np
        HEAD_NUM = 16
        B, S, D = x.shape
        H = HEAD_NUM
        hd = D // H

        def proj(W, b):
            return (x @ W.T + b).reshape(B, S, H, hd).transpose(0, 2, 1, 3)
        Q, K, V = (proj(Wq, bq), proj(Wk, bk), proj(Wv, bv))
        scale = 1.0 / jnp.sqrt(jnp.float32(hd))
        scores = jnp.einsum('bhqd,bhkd->bhqk', Q, K) * scale
        attn = jax.nn.softmax(scores, axis=-1)
        out = jnp.einsum('bhqk,bhkd->bhqd', attn, V)
        out = out.transpose(0, 2, 1, 3).reshape(B, S, D)
        return out @ Wo.T + bo

    def _L0_ffn_ref(tgt, Wr, br, W1, b1, W2, b2, gamma, beta):
        import jax, jax.numpy as jnp
        import numpy as np
        B, S, D, F, E = (2, 256, 128, 512, 8)
        LN_EPS = 1e-05

        def _layer_norm(x, gamma, beta):
            mu = jnp.mean(x, axis=-1, keepdims=True)
            var = jnp.mean(jnp.square(x - mu), axis=-1, keepdims=True)
            return (x - mu) * jax.lax.rsqrt(var + LN_EPS) * gamma + beta
        logits = jnp.einsum('bsd,ed->bse', tgt, Wr) + br
        top_v, top_i = jax.lax.top_k(logits, 2)
        top_w = jax.nn.softmax(top_v, axis=-1)
        n_exp = logits.shape[-1]
        router_w = jnp.sum(jax.nn.one_hot(top_i, n_exp, dtype=top_w.dtype) * top_w[..., None], axis=-2)
        h = jnp.einsum('bsd,efd->bsef', tgt, W1) + b1
        h = jax.nn.relu(h)
        o = jnp.einsum('bsef,edf->bsed', h, W2) + b2
        tgt2 = jnp.einsum('bsed,bse->bsd', o, router_w)
        return _layer_norm(tgt + tgt2, gamma, beta)
    x = L0_attn_x
    x = x + _L0_attn_ref(_layernorm(x, axis=-1), L0_attn_Wq, L0_attn_bq, L0_attn_Wk, L0_attn_bk, L0_attn_Wv, L0_attn_bv, L0_attn_Wo, L0_attn_bo)
    x = x + _L0_ffn_ref(_layernorm(x, axis=-1), L0_ffn_Wr, L0_ffn_br, L0_ffn_W1, L0_ffn_b1, L0_ffn_W2, L0_ffn_b2, L0_ffn_gamma, L0_ffn_beta)
    return x

_drawn_inputs = setup_inputs


def setup_inputs(seed=0):
    import zlib

    import numpy as np

    out = dict(_drawn_inputs(seed))
    spreads = {'L0_attn_bq': (0.0, 0.478),
     'L0_attn_bk': (0.0, 0.8),
     'L0_attn_bv': (0.0, 0.1),
     'L0_attn_bo': (0.0, 0.1),
     'L0_ffn_br': (0.0, 0.1),
     'L0_ffn_b1': (0.0, 0.1),
     'L0_ffn_b2': (0.0, 0.1),
     'L0_ffn_gamma': (1.0, 0.2),
     'L0_ffn_beta': (0.0, 0.1)}
    factors = {}
    for name, (base, spread) in spreads.items():
        noise = np.random.default_rng([zlib.crc32(name.encode()), seed]).standard_normal(out[name].shape)
        drawn = base * np.exp(spread * noise) if base else spread * noise
        out[name] = jnp.asarray(drawn.astype(out[name].dtype))
    for name, factor in factors.items():
        out[name] = (out[name] * factor).astype(out[name].dtype)
    return out
```

```python
from contextlib import ExitStack

import numpy as np

import concourse.bass as bass
from concourse import mybir

ALU = mybir.AluOpType
ACT = mybir.ActivationFunctionType
F32 = mybir.dt.float32
F32R = mybir.dt.float32r
U32 = mybir.dt.uint32
AX_X = mybir.AxisListType.X
ds = bass.ds

P = 128
B, S, D = 8, 512, 128
H = 16
HD = D // H
TILES = S // P
QUADS = H // 4
GROUPS = QUADS * TILES
E = 8
F = 512
FC = F // P
CH = 9 + 2 * E + 3
SCALE = float(np.float32(1.0) / np.sqrt(np.float32(HD)))
EPS = 1e-5

SCORE_ROWS = 3 * HD
SHIFT_ROW = SCORE_ROWS
ST_LAG = 5
PV_LAG = 7
FIRST_BEAT = -12
LAST_BEAT = GROUPS * (B - 1) + 33
LOOP_FROM = 18
LOOPS = 6
ST_BANKS = 3
PT_SLOTS = 4


def st_bank(k):
    k %= 4 * GROUPS
    return 1 if k == 4 * GROUPS - 1 else k % ST_BANKS


def st_bank_last_user(k):
    j = k - 1
    while st_bank(j) != st_bank(k):
        j -= 1
    return j


def side_task(T):
    if T % 4 == 0:
        kind, of, n = "V", (T + 4) // 4, QUADS * B
    elif T % 4 == 2:
        kind, of, n = "K", (T + 6) // 4, QUADS * B
    elif T % 4 == 3:
        kind, of, n = "Q", (T + 5) // 4, QUADS * B
    elif T % GROUPS == 9:
        kind, of, n = "XT", (T + 7) // GROUPS, B
    elif T % GROUPS == 13:
        kind, of, n = "OT", (T - 29) // GROUPS, B
    elif T % GROUPS == 1:
        kind, of, n = "O", (T - 33) // GROUPS, B
    else:
        return None
    return (kind, of) if 0 <= of < n else None


SIDE = {}
for _T in range(FIRST_BEAT, LAST_BEAT + 1):
    if side_task(_T):
        SIDE[side_task(_T)] = len(SIDE)


class Beat:

    def __init__(self, T, turn=0):
        self.T, self.turn = T, turn

    def scores(self):
        return self.T if 0 <= self.T < GROUPS * B else None

    def st(self):
        n = self.T - ST_LAG
        return n if 0 <= n < GROUPS * B else None

    def pv(self):
        n = self.T - PV_LAG
        return n if 0 <= n < GROUPS * B else None

    def every(self, period, offset, count):
        n, r = divmod(self.T - offset, period)
        return n if r == 0 and 0 <= n < count else None

    def wait(self, eng, sem, count, per_batch):
        if isinstance(self.turn, int):
            if count > 0:
                eng.wait_ge(sem, count)
        else:
            eng.wait_ge(sem, self.turn * per_batch + count)


def beats(eng, body):
    for T in range(FIRST_BEAT, LOOP_FROM):
        body(Beat(T))
    with eng.Fori(0, LOOPS) as turn:
        for T in range(LOOP_FROM, LOOP_FROM + GROUPS):
            body(Beat(T, turn))
    for T in range(LOOP_FROM + GROUPS * LOOPS, LAST_BEAT + 1):
        body(Beat(T))


def layer(nc, x, Wq, bq, Wk, bk, Wv, bv, Wo, bo, Wr, br, W1, b1, W2, b2, gamma, beta, out):
    with ExitStack() as whole:
        xres = whole.enter_context(nc.sbuf_tensor("xres", [P, B * TILES, D], F32))
        ident = whole.enter_context(nc.sbuf_tensor("ident", [P, P], F32))
        attention(nc, x, Wq, bq, Wk, bk, Wv, bv, Wo, bo, xres, ident)
        experts(nc, Wr, br, W1, b1, W2, b2, gamma, beta, xres, ident, out)


def attention(nc, x, Wq, bq, Wk, bk, Wv, bv, Wo, bo, xres, ident):
    with ExitStack() as ctx:
        def sb(name, shape, dt=F32):
            return ctx.enter_context(nc.sbuf_tensor(name, shape, dt))

        def sem(name):
            return ctx.enter_context(nc.semaphore(name))

        def psum(name, banks=1):
            return ctx.enter_context(nc.psum_tensor(name, [P, banks, 512], F32))

        xall = sb("xall", [P, B * TILES, D])
        qst = sb("qst", [P, S])
        qs = [sb(f"qs{v}", [P, QUADS, S], F32R) for v in range(2)]
        kst = sb("kst", [P, QUADS, S], F32R)
        vst = sb("vst", [P, TILES, H, 32])
        pt = sb("pt", [P, PT_SLOTS, 4, S])
        pvs = sb("pvs", [P, 2, S])
        onorm = sb("onorm", [P, TILES, D])
        rden = sb("rden", [P, TILES, 4])
        mneg = sb("mneg", [P, 2, TILES, P])
        xn = sb("xn", [P, TILES, D])
        xth, xtl = sb("xth", [P, S], F32R), sb("xtl", [P, S], F32R)
        oth, otl = sb("oth", [P, S], F32R), sb("otl", [P, S], F32R)
        hm = sb("hm", [P, S], F32R)
        stats = sb("stats", [P, TILES, 6])
        moments = sb("moments", [P, TILES, 2])
        vareps = sb("vareps", [P, TILES])
        rstd = sb("rstd", [P, TILES])
        power = sb("power", [P, TILES])
        eps = sb("eps", [P, TILES])
        wraw = sb("wraw", [P, 4, D])
        wh = sb("wh", [P, 2, QUADS, P], F32R)
        wl = sb("wl", [P, 2, QUADS, P], F32R)
        wvh, wvl = sb("wvh", [P, D], F32R), sb("wvl", [P, D], F32R)
        woh, wol = sb("woh", [P, D], F32R), sb("wol", [P, D], F32R)
        rows = sb("rows", [1, 4, D])
        brow = sb("brow", [1, 2, QUADS, P])
        mrow = sb("mrow", [1, 4, P])
        ones = sb("ones", [1, P])
        bcol = sb("bcol", [P, 2 * QUADS + 4])
        bmask = sb("bmask", [P, 2 * QUADS])
        bvb = sb("bvb", [P, D])
        bob = sb("bob", [P, D])

        s_psum = psum("s_psum", 2)
        st_psum = psum("st_psum", ST_BANKS)
        pv_psum = psum("pv_psum")
        turn_psum = psum("turn_psum")
        side_psum = psum("side_psum")

        w_loaded, b_loaded, x0_loaded, x_loaded = (sem(n) for n in ("w_loaded", "b_loaded", "x0_loaded", "x_loaded"))
        ident_zero, ident_ready, consts_ready, pool_consts = (
            sem(n) for n in ("ident_zero", "ident_ready", "consts_ready", "pool_consts"))
        rows_ready, w_turned, w_high, w_ready = (sem(n) for n in ("rows_ready", "w_turned", "w_high", "w_ready"))
        cols_made, cols_ready, setup_used = (sem(n) for n in ("cols_made", "cols_ready", "setup_used"))
        stats_done, moments_done, vareps_done, rstd_done, xn_done = (
            sem(n) for n in ("stats_done", "moments_done", "vareps_done", "rstd_done", "xn_done"))
        s_made, max_done, shift_turned, shift_added = (
            sem(n) for n in ("s_made", "max_done", "shift_turned", "shift_added"))
        st_made, exp_done, pv_made, pv_copied = (sem(n) for n in ("st_made", "exp_done", "pv_made", "pv_copied"))
        o_turned, rden_done, o_normed = (sem(n) for n in ("o_turned", "rden_done", "o_normed"))
        side_made, side_high, side_done = (sem(n) for n in ("side_made", "side_high", "side_done"))
        xbo_done, q_parted = sem("xbo_done"), sem("q_parted")

        block = ctx.enter_context(nc.Block())
        x_tiles = x.rearrange("b (j p) d -> p b j d", p=P)

        @block.sync
        def _(sp):
            sp.dma_start(xall[:, 0:TILES, :], x_tiles[:, 0]).then_inc(x0_loaded, 16)
            for n, w in enumerate((Wk, Wq, Wv, Wo)):
                sp.dma_start(wraw[:, n, :], w).then_inc(w_loaded, 16)
            for n, v in enumerate((bk, bq, bv, bo)):
                sp.dma_start(rows[:, n, :], v.rearrange("(a d) -> a d", a=1)).then_inc(b_loaded, 16)
            for b in range(1, B):
                sp.dma_start(xall[:, TILES * b:TILES * b + TILES, :], x_tiles[:, b]).then_inc(x_loaded, 16)

        @block.gpsimd
        def _(pool):
            nc.gpsimd.memset(ident[:], 0.0).then_inc(ident_zero, 1)
            pool.wait_ge(ident_zero, 1)
            nc.gpsimd.affine_select(out=ident[:], in_=ident[:], compare_op=ALU.not_equal, fill=1.0, base=0,
                                    pattern=[[-1, P]], channel_multiplier=1).then_inc(ident_ready, 1)
            nc.gpsimd.memset(power[:], -0.5).then_inc(pool_consts, 1)
            nc.gpsimd.memset(eps[:], EPS).then_inc(pool_consts, 1)
            nc.gpsimd.memset(mneg[:], 0.0).then_inc(pool_consts, 1)
            nc.gpsimd.memset(vst[:], 0.0).then_inc(pool_consts, 1)
            pool.wait_ge(pool_consts, 4)
            nc.gpsimd.memset(vst[:, :, :, HD:HD + 1], 1.0).then_inc(pool_consts, 1)

            def beat(t):
                if (b := t.every(GROUPS, -11, B)) is not None:
                    t.wait(pool, moments_done, b + 1, 1)
                    nc.gpsimd.tensor_tensor(vareps[:], moments[:, :, 1], eps[:], ALU.add).then_inc(vareps_done, 1)
                    t.wait(pool, vareps_done, b + 1, 1)
                    if b > 0:
                        t.wait(pool, xn_done, b, 1)
                    nc.gpsimd.tensor_tensor(rstd[:], vareps[:], power[:], ALU.pow).then_inc(rstd_done, 1)

            for T in range(FIRST_BEAT, LOOP_FROM):
                beat(Beat(T))
                if T == -1:
                    pool.wait_ge(x0_loaded, 16)
                    pool.wait_ge(x_loaded, 16 * (B - 1))
                    pool.wait_ge(cols_ready, 1)
                    nc.gpsimd.tensor_tensor(
                        xres[:], xall[:], bob[:].unsqueeze(1).to_broadcast([P, B * TILES, D]), ALU.add
                    ).then_inc(xbo_done, 1)
            with pool.Fori(0, LOOPS) as turn:
                for T in range(LOOP_FROM, LOOP_FROM + GROUPS):
                    beat(Beat(T, turn))

        @block.scalar
        def _(act):
            act.wait_ge(consts_ready, 1)
            act.wait_ge(w_turned, 1)
            for n in range(2):
                for r in range(3):
                    nc.scalar.copy(
                        wh[:, n].rearrange("p c (g r d) -> p c g r d", g=4, d=HD)[:, :, :, r, :],
                        side_psum[:, 0, P * n:P * n + P].rearrange("p (c g d) -> p c g d", c=QUADS, d=HD))
            nc.scalar.copy(wvh[:], side_psum[:, 0, 2 * P:3 * P])
            nc.scalar.copy(woh[:], side_psum[:, 0, 3 * P:4 * P]).then_inc(w_high, 1)

            def beat(t):
                if (q := t.every(4, -4, QUADS * B)) is not None:
                    t.wait(act, side_done, SIDE["Q", q] + 1, 15)
                    for v in range(2):
                        nc.scalar.activation(qs[v][:, q % QUADS, :], qst[:], ACT.Copy,
                                             scale=bcol[:, 2 * QUADS + 2 + v:2 * QUADS + 3 + v]).then_inc(q_parted, 1)
                if (q := t.every(4, 11, QUADS * B)) is not None:
                    t.wait(act, pv_made, 4 * q + 4, GROUPS)
                    if q >= 2:
                        t.wait(act, o_turned, q - 1, QUADS)
                    nc.scalar.copy(pvs[:, q % 2, :], pv_psum[:, 0, :]).then_inc(pv_copied, 1)
                n = t.st()
                for g in range(4):
                    if n is not None:
                        k = 4 * n + g
                        t.wait(act, st_made, k + 1, 4 * GROUPS)
                        if n >= PT_SLOTS and g == 0:
                            t.wait(act, pv_made, n - PT_SLOTS + 1, GROUPS)
                        nc.scalar.activation(pt[:, n % PT_SLOTS, g, :], st_psum[:, st_bank(k), :], ACT.Exp,
                                             scale=SCALE).then_inc(exp_done, 1)
                    if g == 1 and side_task(t.T):
                        kind, of = side_task(t.T)
                        i = SIDE[kind, of]
                        if kind in ("K", "Q"):
                            w = 0 if kind == "K" else 1
                            c = of % QUADS
                            col = 2 * QUADS + w
                            t.wait(act, side_made, i + 1, 15)
                            nc.scalar.activation(hm[:], side_psum[:, 0, :], ACT.Identity,
                                                 bias=bmask[:, QUADS * w + c:QUADS * w + c + 1],
                                                 scale=bcol[:, col:col + 1]).then_inc(side_high, 1)
                        elif kind == "XT":
                            t.wait(act, side_made, i + 1, 15)
                            nc.scalar.copy(xth[:], side_psum[:, 0, :]).then_inc(side_high, 1)
                        elif kind == "OT":
                            t.wait(act, side_made, i + 1, 15)
                            nc.scalar.copy(oth[:], side_psum[:, 0, :]).then_inc(side_high, 1)

            act.wait_ge(cols_ready, 1)
            beats(act, beat)


        high_before = {}
        for task, i in sorted(SIDE.items(), key=lambda kv: kv[1]):
            high_before[task] = sum(1 for (kind, _), j in SIDE.items() if j <= i and kind in ("K", "Q", "XT", "OT"))

        @block.vector
        def _(dve):
            nc.vector.memset(wh[:].bitcast(U32), 0)
            nc.vector.memset(wl[:].bitcast(U32), 0)
            nc.vector.memset(brow[:], 0.0)
            nc.vector.memset(mrow[:], 0.0)
            nc.vector.memset(ones[:], 1.0).then_inc(consts_ready, 1)
            dve.wait_ge(consts_ready, 1)
            dve.wait_ge(b_loaded, 64)
            for n in range(2):
                for r in range(3):
                    nc.vector.tensor_copy(
                        brow[:, n].rearrange("p c (g r d) -> p c g r d", g=4, d=HD)[:, :, :, r, :],
                        rows[:, n, :].rearrange("p (c g d) -> p c g d", c=QUADS, d=HD))
            nc.vector.memset(brow[:, 0].rearrange("p c (g r) -> p c g r", g=4)[:, :, :, SHIFT_ROW], 1.0)
            for n, r in ((0, 2), (1, 1)):
                nc.vector.memset(mrow[:, n].rearrange("p (g r) -> p g r", g=4)[:, :, HD * r:HD * r + HD], 1.0)
                nc.vector.memset(mrow[:, 2 + n].rearrange("p (g v r) -> p g v r", g=2, v=2)[:, :, n, :], 1.0)\
                    .then_inc(rows_ready, 1)
            dve.wait_ge(w_high, 1)
            for n in range(2):
                for r in range(3):
                    def stack(w):
                        return w[:, n].rearrange("p c (g r d) -> p c g r d", g=4, d=HD)[:, :, :, r, :]
                    nc.vector.tensor_tensor(
                        stack(wl), side_psum[:, 0, P * n:P * n + P].rearrange("p (c g d) -> p c g d", c=QUADS, d=HD),
                        stack(wh).bitcast(F32), ALU.subtract)
            nc.vector.tensor_tensor(wvl[:], side_psum[:, 0, 2 * P:3 * P], wvh[:].bitcast(F32), ALU.subtract)
            nc.vector.tensor_tensor(wol[:], side_psum[:, 0, 3 * P:4 * P], woh[:].bitcast(F32), ALU.subtract)\
                .then_inc(w_ready, 1)
            dve.wait_ge(cols_made, 1)
            nc.vector.tensor_copy(bcol[:], turn_psum[:, 0, 0:2 * QUADS + 4]).then_inc(setup_used, 1)
            nc.vector.tensor_copy(bvb[:], turn_psum[:, 0, 128:256])
            nc.vector.tensor_copy(bob[:], turn_psum[:, 0, 256:384])
            dve.wait_ge(setup_used, 1)
            for n in range(2):
                ins = nc.vector.tensor_scalar(bmask[:, QUADS * n:QUADS * n + QUADS],
                                              bcol[:, QUADS * n:QUADS * n + QUADS],
                                              bcol[:, 2 * QUADS + n:2 * QUADS + n + 1], None, ALU.mult)
            ins.then_inc(cols_ready, 1)

            def maxima(t, g):
                n = t.scores()
                if n is None:
                    return
                k = 4 * n + g
                t.wait(dve, s_made, k + 1, 4 * GROUPS)
                if n == 0 and g == 0:
                    dve.wait_ge(pool_consts, 5)
                nc.vector.tensor_reduce(mneg[:, (n // 4) % 2, n % 4, 32 * g + SHIFT_ROW:32 * g + SHIFT_ROW + 1],
                                        s_psum[:, k % 2, :], AX_X, ALU.max, negate=True).then_inc(max_done, 1)

            def beat(t):
                if (b := t.every(GROUPS, -11, B)) is not None:
                    t.wait(dve, stats_done, b + 1, 1)
                maxima(t, 0)
                maxima(t, 1)
                if (q := t.every(4, 4, QUADS * B)) is not None:
                    c = q % QUADS
                    t.wait(dve, shift_turned, q + 1, QUADS)
                    for v in range(2):
                        nc.vector.scalar_tensor_tensor(
                            out=qs[v][:, c, :], in0=turn_psum[:, 0, :],
                            scalar=bcol[:, 2 * QUADS + 2 + v:2 * QUADS + 3 + v],
                            in1=qs[v][:, c, :].bitcast(F32), op0=ALU.mult, op1=ALU.add).then_inc(shift_added, 1)
                if (q := t.every(4, 14, QUADS * B)) is not None:
                    c = q % QUADS
                    t.wait(dve, o_turned, q + 1, QUADS)
                    sums = turn_psum[:, 0, :].rearrange("p (j g r) -> p j g r", j=TILES, g=4)
                    nc.vector.reciprocal(rden[:], sums[:, :, :, HD]).then_inc(rden_done, 1)
                    t.wait(dve, rden_done, q + 1, QUADS)
                    nc.vector.tensor_tensor(
                        onorm[:].rearrange("p j (h d) -> p j h d", d=HD)[:, :, 4 * c:4 * c + 4, :],
                        sums[:, :, :, 0:HD], rden[:].unsqueeze(3).to_broadcast([P, TILES, 4, HD]),
                        ALU.mult).then_inc(o_normed, 1)
                maxima(t, 2)
                maxima(t, 3)
                if side_task(t.T):
                    kind, of = side_task(t.T)
                    i = SIDE[kind, of]
                    if kind in ("K", "Q"):
                        c = of % QUADS
                        w, dst = (0, kst[:, c, :]) if kind == "K" else (1, qst[:])
                        if kind == "Q" and of > 0:
                            t.wait(dve, q_parted, 2 * of, 2 * QUADS)
                        t.wait(dve, side_high, high_before[kind, of], 10)
                        nc.vector.scalar_tensor_tensor(
                            out=dst, in0=side_psum[:, 0, :],
                            scalar=bcol[:, QUADS * w + c:QUADS * w + c + 1], in1=hm[:].bitcast(F32),
                            op0=ALU.add, op1=ALU.subtract).then_inc(side_done, 1)
                    elif kind in ("XT", "OT"):
                        hi, lo = (xth, xtl) if kind == "XT" else (oth, otl)
                        t.wait(dve, side_high, high_before[kind, of], 10)
                        nc.vector.tensor_tensor(lo[:], side_psum[:, 0, :], hi[:].bitcast(F32), ALU.subtract)\
                            .then_inc(side_done, 1)
                    elif kind == "V":
                        c = of % QUADS
                        t.wait(dve, side_made, i + 1, 15)
                        if of < QUADS:
                            dve.wait_ge(pool_consts, 5)
                        nc.vector.tensor_tensor(
                            vst[:, :, 4 * c:4 * c + 4, 0:HD],
                            side_psum[:, 0, 0:P].rearrange("p (j g d) -> p j g d", j=TILES, d=HD),
                            bvb[:, 32 * c:32 * c + 32].rearrange("p (g d) -> p g d", d=HD).unsqueeze(1)
                            .to_broadcast([P, TILES, 4, HD]), ALU.add).then_inc(side_done, 1)
                    else:
                        t.wait(dve, side_made, i + 1, 15)
                        if of == 0:
                            dve.wait_ge(xbo_done, 1)
                        at = ds(t.turn * TILES + TILES * of, TILES) if not isinstance(t.turn, int) \
                            else slice(TILES * of, TILES * of + TILES)
                        nc.vector.tensor_tensor(
                            xres[:, at, :], side_psum[:, 0, :].rearrange("p (j d) -> p j d", j=TILES),
                            xres[:, at, :], ALU.add).then_inc(side_done, 1)
                if (b := t.every(GROUPS, -12, B)) is not None:
                    if b == 0:
                        dve.wait_ge(x0_loaded, 16)
                    else:
                        dve.wait_ge(x_loaded, 16 * (B - 1))
                    for j in range(TILES):
                        at = t.turn * TILES + (TILES * b + j)
                        ins = nc.vector.bn_stats(stats[:, j, :], xall[:, ds(at, 1) if not isinstance(at, int)
                                                                     else slice(at, at + 1), :])
                    ins.then_inc(stats_done, 1)
                if t.every(GROUPS, -11, B) is not None:
                    for j in range(TILES):
                        ins = nc.vector.bn_aggr(moments[:, j, :], stats[:, j, :])
                    ins.then_inc(moments_done, 1)
                if (b := t.every(GROUPS, -9, B)) is not None:
                    t.wait(dve, rstd_done, b + 1, 1)
                    for j in range(TILES):
                        at = t.turn * TILES + (TILES * b + j)
                        ins = nc.vector.tensor_scalar(
                            xn[:, j:j + 1, :], xall[:, ds(at, 1) if not isinstance(at, int) else slice(at, at + 1), :],
                            moments[:, j, 0:1], rstd[:, j:j + 1], ALU.subtract, ALU.mult)
                    ins.then_inc(xn_done, 1)

            beats(dve, beat)

        @block.tensor
        def _(pe):
            mm = nc.tensor.matmul

            def split3(dst, ah, al, bh, bl):
                mm(dst, ah, bh, start=True, stop=False)
                mm(dst, al, bh, start=False, stop=False)
                return mm(dst, ah, bl, start=False, stop=True)

            pe.wait_ge(ident_ready, 1)
            pe.wait_ge(w_loaded, 64)
            for n in range(4):
                ins = nc.tensor.transpose(side_psum[:, 0, P * n:P * n + P], wraw[:, n, :], ident[:])
            ins.then_inc(w_turned, 1)
            pe.wait_ge(rows_ready, 2)
            for n in range(2):
                for c in range(QUADS):
                    mm(turn_psum[:, 0, QUADS * n + c:QUADS * n + c + 1], brow[:, n, c, :], ones[:, 0:1],
                       start=True, stop=True)
            for n in range(4):
                mm(turn_psum[:, 0, 2 * QUADS + n:2 * QUADS + n + 1], mrow[:, n, :], ones[:, 0:1], start=True, stop=True)
            for n in (2, 3):
                ins = mm(turn_psum[:, 0, 128 * (n - 1):128 * n], ones[:], rows[:, n, :], start=True, stop=True)
            ins.then_inc(cols_made, 1)
            pe.wait_ge(w_ready, 1)
            pe.wait_ge(cols_ready, 1)

            def scores(t, g):
                n = t.scores()
                if n is None:
                    return
                k, q = 4 * n + g, n // 4
                if n % 4 == 0 and g == 0:
                    t.wait(pe, q_parted, 2 * q + 2, 2 * QUADS)
                if k >= 2:
                    t.wait(pe, max_done, k - 1, 4 * GROUPS)
                r = slice(64 * (g // 2), 64 * (g // 2) + 64)
                mm(s_psum[:, k % 2, :], qs[g % 2][r, q % QUADS, P * (n % 4):P * (n % 4) + P], kst[r, q % QUADS, :],
                   start=True, stop=True).then_inc(s_made, 1)

            def scores_t(t, g):
                n = t.st()
                if n is None:
                    return
                k, q = 4 * n + g, n // 4
                if n % 4 == 0 and g == 0:
                    t.wait(pe, shift_added, 2 * q + 2, 2 * QUADS)
                if st_bank_last_user(k) >= 0:
                    t.wait(pe, exp_done, st_bank_last_user(k) + 1, 4 * GROUPS)
                r = slice(64 * (g // 2), 64 * (g // 2) + 64)
                mm(st_psum[:, st_bank(k), :], kst[r, q % QUADS, P * (n % 4):P * (n % 4) + P], qs[g % 2][r, q % QUADS, :],
                   start=True, stop=True).then_inc(st_made, 1)

            def turn(t):
                if (q := t.every(4, 4, QUADS * B)) is not None:
                    t.wait(pe, max_done, 16 * q + 16, 4 * GROUPS)
                    if q - 2 > 0:
                        t.wait(pe, o_normed, q - 2, QUADS)
                    for j in range(TILES):
                        ins = nc.tensor.transpose(turn_psum[:, 0, P * j:P * j + P], mneg[:, q % 2, j, :], ident[:])
                    ins.then_inc(shift_turned, 1)
                if (q := t.every(4, 14, QUADS * B)) is not None:
                    t.wait(pe, pv_copied, q + 1, QUADS)
                    if q + 3 <= QUADS * B:
                        t.wait(pe, shift_added, 2 * q + 6, 2 * QUADS)
                    else:
                        t.wait(pe, o_normed, q, QUADS)
                    for j in range(TILES):
                        ins = nc.tensor.transpose(turn_psum[:, 0, P * j:P * j + P], pvs[:, q % 2, P * j:P * j + P],
                                                  ident[:])
                    ins.then_inc(o_turned, 1)

            def side(t):
                if not side_task(t.T):
                    return
                kind, of = side_task(t.T)
                i = SIDE[kind, of]
                t.wait(pe, side_done, i, 15)
                c = of % QUADS
                if kind == "XT":
                    t.wait(pe, xn_done, of + 1, 1)
                    for j in range(TILES):
                        ins = nc.tensor.transpose(side_psum[:, 0, P * j:P * j + P], xn[:, j, :], ident[:])
                elif kind in ("K", "Q"):
                    w = 0 if kind == "K" else 1
                    ins = split3(side_psum[:, 0, :], wh[:, w, c, :], wl[:, w, c, :], xth[:], xtl[:])
                elif kind == "V":
                    for j in range(TILES):
                        ins = split3(side_psum[:, 0, 32 * j:32 * j + 32], xth[:, P * j:P * j + P],
                                     xtl[:, P * j:P * j + P], wvh[:, 32 * c:32 * c + 32], wvl[:, 32 * c:32 * c + 32])
                elif kind == "OT":
                    t.wait(pe, o_normed, QUADS * (of + 1), QUADS)
                    for j in range(TILES):
                        ins = nc.tensor.transpose(side_psum[:, 0, P * j:P * j + P], onorm[:, j, :], ident[:])
                else:
                    for j in range(TILES):
                        ins = split3(side_psum[:, 0, P * j:P * j + P], oth[:, P * j:P * j + P],
                                     otl[:, P * j:P * j + P], woh[:], wol[:])
                ins.then_inc(side_made, 1)

            def values(t):
                n = t.pv()
                if n is None:
                    return
                q = n // 4
                t.wait(pe, exp_done, 4 * n + 4, 4 * GROUPS)
                if n % 4 == 0:
                    t.wait(pe, side_done, SIDE["V", q] + 1, 15)
                    if q > 0:
                        t.wait(pe, pv_copied, q, QUADS)
                for g in range(4):
                    ins = mm(pv_psum[32 * g:32 * g + 32, 0, :], vst[:, n % 4, 4 * (q % QUADS) + g, :],
                             pt[:, n % PT_SLOTS, g, :], start=(n % 4 == 0), stop=(n % 4 == 3))
                ins.then_inc(pv_made, 1)

            def beat(t):
                scores(t, 0)
                scores(t, 1)
                turn(t)
                scores_t(t, 0)
                scores_t(t, 1)
                side(t)
                scores(t, 2)
                scores(t, 3)
                scores_t(t, 2)
                scores_t(t, 3)
                values(t)

            beats(pe, beat)


def experts(nc, Wr, br, W1, b1, W2, b2, gamma, beta, xres, ident, out):
    with ExitStack() as ctx:
        def sb(name, shape, dt=F32):
            return ctx.enter_context(nc.sbuf_tensor(name, shape, dt))

        def sem(name):
            return ctx.enter_context(nc.semaphore(name))

        def psum(name, banks=1):
            return ctx.enter_context(nc.psum_tensor(name, [P, banks, 512], F32))

        w1raw = sb("w1raw", [P, E * FC, D])
        w2raw = sb("w2raw", [P, E, F])
        w1h = sb("w1h", [P, E * FC, P], F32R)
        w1l = sb("w1l", [P, E * FC, P], F32R)
        w2t = sb("w2t", [P, E * FC, D])
        wrraw = sb("wrraw", [E, D])
        wrt = sb("wrt", [P, E])
        b1raw = sb("b1raw", [E * FC, P])
        b1c = sb("b1c", [P, E * FC])
        rows2 = sb("rows2", [1, 2 * D + E + E * D])
        rowsb = sb("rowsb", [P, 2 * D + E + E * D])
        ones2 = sb("ones2", [1, P])
        iota8 = sb("iota8", [P, E])
        eps2 = sb("eps2", [P, TILES])
        power2 = sb("power2", [P, TILES])
        st2 = sb("st2", [P, TILES, 6])
        mv2 = sb("mv2", [P, TILES, 2])
        ve2 = sb("ve2", [P, TILES])
        rs2 = sb("rs2", [P, TILES])
        acc = sb("acc", [P, TILES, D])
        xtf = sb("xtf", [P, S])
        xth = sb("xth2", [P, S], F32R)
        xtl = sb("xtl2", [P, S], F32R)
        lg = sb("lg", [P, TILES, E])
        m8 = sb("m8", [P, TILES, 8])
        i8 = sb("i8", [P, TILES, 8], U32)
        i2 = sb("i2", [P, TILES, 2])
        dv = sb("dv", [P, TILES])
        ev = sb("ev", [P, TILES])
        sv = sb("sv", [P, TILES])
        w12 = sb("w12", [P, TILES, 2])
        oh = sb("oh", [P, TILES, 2, E])
        rw = sb("rw", [P, TILES, E])
        h = sb("h", [P, FC, S])
        yb = sb("yb", [P, TILES, D])
        cx_t = sb("cx_t", [P, 8])
        fin = sb("fin", [P, TILES, D])
        hp = psum("hp", 3)
        op = psum("op", 2)
        tp = psum("tp", 2)
        ld, cst, dch, pch, ach, mch = (sem(n) for n in ("ld", "cst", "dch", "pch", "ach", "mch"))
        wtp, wth, wtd, stored = (sem(n) for n in ("wtp", "wth", "wtd", "stored"))
        lnv, lnr = sem("lnv"), sem("lnr")
        xnd, xtp, xta, xtd, rtp, rtd, evd, sd, rwd = (sem(n) for n in ("xnd", "xtp", "xta", "xtd", "rtp", "rtd", "evd", "sd", "rwd"))
        hm_, hr, om, oa, finr, chain = (sem(n) for n in ("hm_", "hr", "om", "oa", "finr", "chain"))
        xns, xs2, cx = sem("xns"), sem("xs2"), sem("cx")
        block = ctx.enter_context(nc.Block())

        @block.sync
        def _(sp):
            sp.dma_start(w1raw[:], W1.rearrange("e (c p) d -> p (e c) d", p=P)).then_inc(ld, 16)
            sp.dma_start(w2raw[:], W2.rearrange("e p f -> p e f")).then_inc(ld, 16)
            sp.dma_start(wrraw[:], Wr).then_inc(ld, 16)
            sp.dma_start(b1raw[:], b1.rearrange("e (c p) -> (e c) p", p=P)).then_inc(ld, 16)
            sp.dma_start(rows2[:, 0:D], gamma.rearrange("(a d) -> a d", a=1)).then_inc(ld, 16)
            sp.dma_start(rows2[:, D:2 * D], beta.rearrange("(a d) -> a d", a=1)).then_inc(ld, 16)
            sp.dma_start(rows2[:, 2 * D:2 * D + E], br.rearrange("(a d) -> a d", a=1)).then_inc(ld, 16)
            sp.dma_start(rows2[:, 2 * D + E:], b2.rearrange("(a e) d -> a (e d)", a=1)).then_inc(stored, 16)
            with sp.Fori(0, B) as i:
                sp.wait_ge(finr, i + 1)
                sp.dma_start(out.rearrange("b (j p) d -> p b j d", p=P)[:, ds(i, 1)], fin[:].unsqueeze(1)).then_inc(stored, 16)
            sp.wait_ge(stored, 16 * B + 16)

        @block.gpsimd
        def _(pool):
            nc.gpsimd.memset(eps2[:], EPS).then_inc(pch, 1)
            nc.gpsimd.memset(power2[:], -0.5).then_inc(pch, 1)
            nc.gpsimd.iota(iota8[:], [[1, E]], base=0, channel_multiplier=0, allow_small_or_imprecise_dtypes=True).then_inc(pch, 1)
            pool.wait_ge(pch, 3)
            with pool.Fori(0, 2 * B) as i:
                pool.wait_ge(lnv, i + 1)
                nc.gpsimd.tensor_tensor(ve2[:], mv2[:, :, 1], eps2[:], ALU.add).then_inc(lnr, 1)
                pool.wait_ge(lnr, i * 2 + 1)
                nc.gpsimd.tensor_tensor(rs2[:], ve2[:], power2[:], ALU.pow).then_inc(lnr, 1)

        @block.scalar
        def _(act):
            for n in range(2 * E):
                act.wait_ge(wtp, n + 1)
                if n < E:
                    nc.scalar.copy(w1h[:, FC * n:FC * n + FC, :], tp[:, n % 2].rearrange("p (c d) -> p c d", c=FC)).then_inc(wth, 1)
                else:
                    nc.scalar.copy(w2t[:, FC * (n - E):FC * (n - E) + FC, :], tp[:, n % 2].rearrange("p (c d) -> p c d", c=FC)).then_inc(wth, 1)
            with act.Fori(0, B) as i:
                act.wait_ge(xtp, i + 1)
                nc.scalar.copy(xth[:], tp[:, 0]).then_inc(xta, 1)
                nc.scalar.copy(xtf[:], tp[:, 0]).then_inc(xta, 1)
                act.wait_ge(rtd, i + 1)
                nc.scalar.activation(ev[:], dv[:], ACT.Exp).then_inc(evd, 1)
                for e in range(E):
                    for f in range(FC):
                        k = FC * e + f
                        act.wait_ge(hm_, i * (E * FC) + (k + 1))
                        if k >= FC:
                            act.wait_ge(om, i * E + e)
                        nc.scalar.activation(h[:, f, :], hp[:, k % 3 if k < 30 else k - 30 + 1], ACT.Relu, bias=b1c[:, k:k + 1]).then_inc(hr, 1)

        @block.vector
        def _(dve):
            nc.vector.memset(ones2[:], 1.0).then_inc(cst, 1)
            for n in range(E):
                dve.wait_ge(wth, n + 1)
                nc.vector.tensor_tensor(w1l[:, FC * n:FC * n + FC, :], tp[:, n % 2].rearrange("p (c d) -> p c d", c=FC),
                                        w1h[:, FC * n:FC * n + FC, :].bitcast(F32), ALU.subtract).then_inc(wtd, 1)
            dve.wait_ge(mch, 1)
            nc.vector.tensor_copy(b1c[:], hp[:, 0, 0:E * FC])
            nc.vector.tensor_copy(wrt[:], hp[:, 0, 64:64 + E])
            for n in range(3):
                w = min(512, 2 * D + E + E * D - 512 * n)
                ins = nc.vector.tensor_copy(rowsb[:, 512 * n:512 * n + w], [hp[:, 1], hp[:, 2], op[:, 0]][n][:, 0:w])
            ins.then_inc(wtd, 1)
            nch = [0]
            ncx = [0]
            i = None

            def link(ins):
                nch[0] += 1
                ins.then_inc(chain, 1)
                dve.wait_ge(chain, i * CH + nch[0])

            def lnorm(src, n):
                for j in range(TILES):
                    ins = nc.vector.bn_stats(st2[:, j, :], src(j))
                ins.then_inc(xns, 1)
                dve.wait_ge(xns, i * 2 + (n + 1))
                nc.vector.tensor_copy(cx_t[:, ncx[0]:ncx[0] + 1], eps2[:, 0:1])
                ncx[0] += 1
                for j in range(TILES):
                    ins = nc.vector.bn_aggr(mv2[:, j, :], st2[:, j, :])
                ins.then_inc(lnv, 1)
                dve.wait_ge(lnr, i * 4 + (2 * n + 2))

            dve.wait_ge(pch, 3)
            with dve.Fori(0, B) as i:
                nch[0] = 0
                lnorm(lambda j: xres[:, ds(i * TILES + j, 1), :], 0)
                for j in range(TILES):
                    ins = nc.vector.tensor_scalar(acc[:, j:j + 1, :], xres[:, ds(i * TILES + j, 1), :], mv2[:, j, 0:1], rs2[:, j:j + 1], ALU.subtract, ALU.mult)
                ins.then_inc(xnd, 1)
                dve.wait_ge(xta, i * 2 + 2)
                nc.vector.tensor_tensor(xtl[:], tp[:, 0], xth[:].bitcast(F32), ALU.subtract).then_inc(xtd, 1)
                dve.wait_ge(rtp, i + 1)
                link(nc.vector.tensor_tensor(lg[:], tp[:, 1, 0:TILES * E].rearrange("p (j e) -> p j e", e=E),
                                             rowsb[:, 2 * D:2 * D + E].unsqueeze(1).to_broadcast([P, TILES, E]), ALU.add))
                nc.vector.tensor_copy(cx_t[:, ncx[0]:ncx[0] + 1], eps2[:, 0:1])
                ncx[0] += 1
                for j in range(TILES):
                    ins = nc.vector.max(m8[:, j, :], lg[:, j, :])
                link(ins)
                nc.vector.tensor_tensor(dv[:], m8[:, :, 1], m8[:, :, 0], ALU.subtract).then_inc(rtd, 1)
                nc.vector.tensor_copy(cx_t[:, ncx[0]:ncx[0] + 1], eps2[:, 0:1])
                ncx[0] += 1
                for j in range(TILES):
                    ins = nc.vector.max_index(i8[:, j, :], m8[:, j, :], lg[:, j, :])
                link(ins)
                link(nc.vector.tensor_copy(i2[:], i8[:, :, 0:2]))
                nc.vector.tensor_tensor(oh[:], iota8[:].unsqueeze(1).unsqueeze(1).to_broadcast([P, TILES, 2, E]),
                                        i2[:].unsqueeze(3).to_broadcast([P, TILES, 2, E]), ALU.is_equal)
                dve.wait_ge(evd, i + 1)
                link(nc.vector.tensor_scalar_add(sv[:], ev[:], 1.0))
                link(nc.vector.reciprocal(w12[:, :, 0], sv[:]))
                link(nc.vector.tensor_tensor(w12[:, :, 1], w12[:, :, 0], ev[:], ALU.mult))
                link(nc.vector.tensor_tensor(oh[:], oh[:], w12[:].unsqueeze(3).to_broadcast([P, TILES, 2, E]), ALU.mult))
                link(nc.vector.tensor_tensor(rw[:], oh[:, :, 0, :], oh[:, :, 1, :], ALU.add))
                for e in range(E):
                    dve.wait_ge(om, i * E + (e + 1))
                    link(nc.vector.tensor_tensor(yb[:], op[:, e % 2].rearrange("p (j d) -> p j d", j=TILES),
                                                 rowsb[:, 2 * D + E + D * e:2 * D + E + D * (e + 1)].unsqueeze(1).to_broadcast([P, TILES, D]), ALU.add))
                    for j in range(TILES):
                        ins = nc.vector.scalar_tensor_tensor(out=acc[:, j, :], in0=yb[:, j, :], scalar=rw[:, j, e:e + 1], in1=acc[:, j, :],
                                                             op0=ALU.mult, op1=ALU.add)
                    link(ins)
                lnorm(lambda j: acc[:, j, :], 1)
                for j in range(TILES):
                    ins = nc.vector.tensor_scalar(acc[:, j, :], acc[:, j, :], mv2[:, j, 0:1], rs2[:, j:j + 1], ALU.subtract, ALU.mult)
                link(ins)
                link(nc.vector.tensor_tensor(acc[:], acc[:], rowsb[:, 0:D].unsqueeze(1).to_broadcast([P, TILES, D]), ALU.mult))
                link(nc.vector.tensor_tensor(acc[:], acc[:], rowsb[:, D:2 * D].unsqueeze(1).to_broadcast([P, TILES, D]), ALU.add))
                dve.wait_ge(stored, i * 16 + 16)
                nc.vector.tensor_tensor(fin[:], acc[:], xres[:, ds(i * TILES, TILES), :], ALU.add).then_inc(finr, 1)
            assert nch[0] == CH, nch

        @block.tensor
        def _(pe):
            mm = nc.tensor.matmul
            pe.wait_ge(ld, 16 * 7)
            pe.wait_ge(stored, 16)
            pe.wait_ge(cst, 1)
            for n in range(2 * E):
                if n >= 2:
                    pe.wait_ge(wth, n - 1)
                    pe.wait_ge(wtd, min(n - 1, E))
                for c in range(FC):
                    src = w1raw[:, FC * n + c, :] if n < E else w2raw[:, n - E, P * c:P * c + P]
                    ins = nc.tensor.transpose(tp[:, n % 2, P * c:P * c + P], src, ident[:])
                ins.then_inc(wtp, 1)
            nc.tensor.transpose(hp[:, 0, 0:E * FC], b1raw[:], ident[0:E * FC, 0:E * FC])
            nc.tensor.transpose(hp[:, 0, 64:64 + E], wrraw[:], ident[0:E, 0:E])
            for n in range(3):
                w = min(512, 2 * D + E + E * D - 512 * n)
                ins = mm([hp[:, 1], hp[:, 2], op[:, 0]][n][:, 0:w], ones2[:], rows2[:, 512 * n:512 * n + w], start=True, stop=True)
            ins.then_inc(mch, 1)
            pe.wait_ge(wth, 2 * E)
            pe.wait_ge(wtd, E + 1)
            with pe.Fori(0, B) as i:
                pe.wait_ge(xnd, i + 1)
                for j in range(TILES):
                    ins = nc.tensor.transpose(tp[:, 0, P * j:P * j + P], acc[:, j, :], ident[:])
                ins.then_inc(xtp, 1)
                pe.wait_ge(xtd, i + 1)
                for j in range(TILES):
                    ins = mm(tp[:, 1, E * j:E * j + E], xtf[:, P * j:P * j + P], wrt[:], start=True, stop=True)
                ins.then_inc(rtp, 1)
                for e in range(E):
                    for f in range(FC):
                        k = FC * e + f
                        bank = k % 3 if k < 30 else k - 30 + 1
                        if k > 2:
                            pe.wait_ge(hr, i * (E * FC) + (k - 2 if k < 30 else k - 1))
                        mm(hp[:, bank], w1h[:, k, :], xth[:], start=True, stop=False)
                        mm(hp[:, bank], w1h[:, k, :], xtl[:], start=False, stop=False)
                        mm(hp[:, bank], w1l[:, k, :], xth[:], start=False, stop=True).then_inc(hm_, 1)
                    pe.wait_ge(hr, i * (E * FC) + FC * (e + 1))
                    if e >= 2:
                        pe.wait_ge(chain, i * CH + (9 + 2 * (e - 2) + 1))
                    for j in range(TILES):
                        for f in range(FC):
                            ins = mm(op[:, e % 2, P * j:P * j + P], h[:, f, P * j:P * j + P], w2t[:, FC * e + f, :], start=(f == 0), stop=(f == FC - 1))
                    ins.then_inc(om, 1)


_INS = ["L0_attn_x", "L0_attn_Wq", "L0_attn_bq", "L0_attn_Wk", "L0_attn_bk", "L0_attn_Wv", "L0_attn_bv",
        "L0_attn_Wo", "L0_attn_bo", "L0_ffn_Wr", "L0_ffn_br", "L0_ffn_W1", "L0_ffn_b1", "L0_ffn_W2",
        "L0_ffn_b2", "L0_ffn_gamma", "L0_ffn_beta"]


def kernel(**inputs):
    import numpy as _np
    import concourse.bacc as _bacc
    from concourse import mybir as _mybir
    from concourse.bass_utils import run_bass_kernel_spmd as _run

    nc = _bacc.Bacc("TRN2", target_bir_lowering=False, num_devices=1)
    arrays, args = {}, []
    for name in _INS:
        a = _np.ascontiguousarray(inputs[name])
        arrays[f"in_{name}_dram"] = a
        args.append(nc.dram_tensor(f"in_{name}_dram", a.shape, _mybir.dt.from_np(a.dtype), kind="ExternalInput").ap())
    args.append(nc.dram_tensor("out_0_dram", (B, S, D), _mybir.dt.float32, kind="ExternalOutput").ap())
    layer(nc, *args)
    r = _run(nc, [arrays], core_ids=[0])
    return r.results[0]["out_0_dram"]
```

```python
from contextlib import ExitStack

import numpy as np

import concourse.bass as bass
from concourse import mybir

ALU = mybir.AluOpType
ACT = mybir.ActivationFunctionType
F32 = mybir.dt.float32
F32R = mybir.dt.float32r
U32 = mybir.dt.uint32
I32 = mybir.dt.int32
AX_X = mybir.AxisListType.X
ds = bass.ds

P = 128
B, S, D = 8, 512, 128
H = 16
HD = D // H
TILES = S // P
QUADS = H // 4
GROUPS = QUADS * TILES
E = 8
F = 512
FC = F // P
N = B * S
HALVES = 2
SLOTS = HALVES * P
REGION = N + SLOTS
ROW = D + 4
NOWHERE = 1 << 20
SCALE = float(np.float32(1.0) / np.sqrt(np.float32(HD)))
EPS = 1e-5

SCORE_ROWS = 3 * HD
SHIFT_ROW = SCORE_ROWS
ST_LAG = 5
PV_LAG = 7
FIRST_BEAT = -11
LAST_BEAT = GROUPS * (B - 1) + 45
LOOP_FROM = 37
LOOPS = 5
SIDES = 16
HIGHS = 10
ST_BANKS = 3
PT_SLOTS = 4


def st_bank(k):
    k %= 4 * GROUPS
    return 1 if k == 4 * GROUPS - 1 else k % ST_BANKS


def st_bank_last_user(k):
    j = k - 1
    while st_bank(j) != st_bank(k):
        j -= 1
    return j


def side_task(T):
    if T % 4 == 0:
        kind, of, n = "V", (T + 4) // 4, QUADS * B
    elif T % 4 == 2:
        kind, of, n = "K", (T + 6) // 4, QUADS * B
    elif T % 4 == 3:
        kind, of, n = "Q", (T + 5) // 4, QUADS * B
    elif T % GROUPS == 9:
        kind, of, n = "XT", (T + 7) // GROUPS, B
    elif T % GROUPS == 13:
        kind, of, n = "OT", (T - 29) // GROUPS, B
    elif T % GROUPS == 1:
        kind, of, n = "O", (T - 33) // GROUPS, B
    else:
        kind, of, n = "X2T", (T - 37) // GROUPS, B
    return (kind, of) if 0 <= of < n else None


SIDE = {}
for _T in range(FIRST_BEAT, LAST_BEAT + 1):
    if side_task(_T):
        SIDE[side_task(_T)] = len(SIDE)


class Beat:

    def __init__(self, T, turn=0):
        self.T, self.turn = T, turn

    def scores(self):
        return self.T if 0 <= self.T < GROUPS * B else None

    def st(self):
        n = self.T - ST_LAG
        return n if 0 <= n < GROUPS * B else None

    def pv(self):
        n = self.T - PV_LAG
        return n if 0 <= n < GROUPS * B else None

    def tiles(self, b, j=0, count=TILES):
        at = TILES * b + j
        return slice(at, at + count) if isinstance(self.turn, int) else ds(self.turn * TILES + at, count)

    def every(self, period, offset, count):
        n, r = divmod(self.T - offset, period)
        return n if r == 0 and 0 <= n < count else None

    def wait(self, eng, sem, count, per_batch):
        if isinstance(self.turn, int):
            if count > 0:
                eng.wait_ge(sem, count)
        else:
            eng.wait_ge(sem, self.turn * per_batch + count)


def beats(eng, body):
    for T in range(FIRST_BEAT, LOOP_FROM):
        body(Beat(T))
    with eng.Fori(0, LOOPS) as turn:
        for T in range(LOOP_FROM, LOOP_FROM + GROUPS):
            body(Beat(T, turn))
    for T in range(LOOP_FROM + GROUPS * LOOPS, LAST_BEAT + 1):
        body(Beat(T))


def layer(nc, x, Wq, bq, Wk, bk, Wv, bv, Wo, bo, Wr, br, W1, b1, W2, b2, gamma, beta, out):
    sent = nc.dram_tensor("sent", (E * REGION, ROW), F32, kind="Internal").ap()
    results = nc.dram_tensor("results", (2 * N, D), F32, kind="Internal").ap()
    with ExitStack() as ctx:
        def sb(name, shape, dt=F32):
            return ctx.enter_context(nc.sbuf_tensor(name, shape, dt))

        kept = Kept(
            xres=sb("xres", [P, B * TILES, D]),
            xn2=sb("xn2", [P, B * TILES, D]),
            ident=sb("ident", [P, P]),
            gates=sb("gates", [P, B * TILES, 2]),
            fill=sb("fill", [P, E]),
            origin=sb("origin", [P, E]),
            w1raw=sb("w1raw", [P, E * FC, D]),
            w2raw=sb("w2raw", [P, E, F]),
            b1raw=sb("b1raw", [E * FC, P]),
            rows=sb("rows2", [1, 2 * D + E * D]))
        attention(nc, x, Wq, bq, Wk, bk, Wv, bv, Wo, bo, Wr, br, W1, b1, W2, b2, gamma, beta, kept, sent)
        experts(nc, kept, sent, results, out)


class Kept:

    def __init__(self, xres, xn2, ident, gates, fill, origin, w1raw, w2raw, b1raw, rows):
        self.xres, self.xn2, self.ident, self.gates = xres, xn2, ident, gates
        self.fill, self.origin, self.rows = fill, origin, rows
        self.w1raw, self.w2raw, self.b1raw = w1raw, w2raw, b1raw


def attention(nc, x, Wq, bq, Wk, bk, Wv, bv, Wo, bo, Wr, br, W1, b1, W2, b2, gamma, beta, kept, sent):
    xres, ident, gates, fill = kept.xres, kept.ident, kept.gates, kept.fill
    with ExitStack() as ctx:
        def sb(name, shape, dt=F32):
            return ctx.enter_context(nc.sbuf_tensor(name, shape, dt))

        def sem(name):
            return ctx.enter_context(nc.semaphore(name))

        def psum(name, banks=1):
            return ctx.enter_context(nc.psum_tensor(name, [P, banks, 512], F32))

        xall = sb("xall", [P, B * TILES, D])
        qst = sb("qst", [P, S])
        qs = [sb(f"qs{v}", [P, QUADS, S], F32R) for v in range(2)]
        kst = sb("kst", [P, QUADS, S], F32R)
        vst = sb("vst", [P, TILES, H, 32])
        pt = sb("pt", [P, PT_SLOTS, 4, S])
        pvs = sb("pvs", [P, 2, S])
        onorm = sb("onorm", [P, TILES, D])
        rden = sb("rden", [P, TILES, 4])
        mneg = sb("mneg", [P, 2, TILES, P])
        xn = sb("xn", [P, TILES, D])
        xth, xtl = sb("xth", [P, S], F32R), sb("xtl", [P, S], F32R)
        oth, otl = sb("oth", [P, S], F32R), sb("otl", [P, S], F32R)
        hm = sb("hm", [P, S], F32R)
        stats = sb("stats", [P, TILES, 6])
        moments = sb("moments", [P, TILES, 2])
        vareps = sb("vareps", [P, TILES])
        rstd = sb("rstd", [P, TILES])
        power = sb("power", [P, TILES])
        eps = sb("eps", [P, TILES])
        wraw = sb("wraw", [P, 4, D])
        wh = sb("wh", [P, 2, QUADS, P], F32R)
        wl = sb("wl", [P, 2, QUADS, P], F32R)
        wvh, wvl = sb("wvh", [P, D], F32R), sb("wvl", [P, D], F32R)
        woh, wol = sb("woh", [P, D], F32R), sb("wol", [P, D], F32R)
        rows = sb("rows", [1, 4, D])
        brrow = sb("brrow", [1, E])
        brow = sb("brow", [1, 2, QUADS, P])
        mrow = sb("mrow", [1, 4, P])
        ones = sb("ones", [1, P])
        bcol = sb("bcol", [P, 2 * QUADS + 4])
        bmask = sb("bmask", [P, 2 * QUADS])
        bvb = sb("bvb", [P, D])
        brb = sb("brb", [P, E])
        wrraw = sb("wrraw", [E, D])
        wrt = sb("wrt", [P, E])
        xt2 = sb("xt2", [P, S])
        xrow = sb("xrow", [P, 2, TILES, ROW])
        stats2 = sb("stats2", [P, TILES, 6])
        moments2 = sb("moments2", [P, TILES, 2])
        vareps2, rstd2 = sb("vareps2", [P, TILES]), sb("rstd2", [P, TILES])
        logits = sb("logits", [P, TILES, E])
        top = sb("top", [P, TILES, 8])
        topi = sb("topi", [P, TILES, 8], U32)
        choice = sb("choice", [P, TILES, 2])
        gap, gexp, gsum = sb("gap", [P, TILES]), sb("gexp", [P, TILES]), sb("gsum", [P, TILES])
        iota8 = sb("iota8", [P, E])
        hot = sb("hot", [P, TILES, 2, E])
        load = sb("load", [P, TILES, E])
        before = sb("before", [P, P])
        ones_sq = sb("ones_sq", [P, P])
        counts = sb("counts", [P, 2, TILES, E])
        start = sb("start", [P, TILES, E])
        place = sb("place", [P, TILES, E])
        picked = sb("picked", [P, TILES, 2, E])
        placef = sb("placef", [P, TILES, 2])
        placeu = sb("placeu", [P, TILES, 2], U32)
        goal = sb("goal", [P, 2, TILES], U32)
        step = sb("step", [P, 2, TILES], U32)
        zero = sb("zero", [P, 2, TILES], U32)
        fence = sb("fence", [P, 2, TILES], U32)
        bob = sb("bob", [P, D])

        s_psum = psum("s_psum", 2)
        st_psum = psum("st_psum", ST_BANKS)
        pv_psum = psum("pv_psum")
        turn_psum = psum("turn_psum")
        side_psum = psum("side_psum")

        w_loaded, b_loaded, x0_loaded, x_loaded = (sem(n) for n in ("w_loaded", "b_loaded", "x0_loaded", "x_loaded"))
        ident_zero, ident_ready, consts_ready, pool_consts = (
            sem(n) for n in ("ident_zero", "ident_ready", "consts_ready", "pool_consts"))
        rows_ready, w_turned, w_high, w_ready = (sem(n) for n in ("rows_ready", "w_turned", "w_high", "w_ready"))
        cols_made, cols_ready, setup_used = (sem(n) for n in ("cols_made", "cols_ready", "setup_used"))
        stats_done, moments_done, vareps_done, rstd_done, xn_done = (
            sem(n) for n in ("stats_done", "moments_done", "vareps_done", "rstd_done", "xn_done"))
        s_made, max_done, shift_turned, shift_added = (
            sem(n) for n in ("s_made", "max_done", "shift_turned", "shift_added"))
        st_made, exp_done, pv_made, pv_copied = (sem(n) for n in ("st_made", "exp_done", "pv_made", "pv_copied"))
        o_turned, rden_done, o_normed = (sem(n) for n in ("o_turned", "rden_done", "o_normed"))
        side_made, side_high, side_done = (sem(n) for n in ("side_made", "side_high", "side_done"))
        xbo_done, q_parted = sem("xbo_done"), sem("q_parted")
        later_loaded = sem("later_loaded")
        stats2_done, moments2_done, vareps2_done, rstd2_done, xn2_done, xn2_kept = (
            sem(n) for n in ("stats2_done", "moments2_done", "vareps2_done", "rstd2_done", "xn2_done", "xn2_kept"))
        logits_made, logits_read, top_done, topi_done, gap_done, gexp_done = (
            sem(n) for n in ("logits_made", "logits_read", "top_done", "topi_done", "gap_done", "gexp_done"))
        choice_done, gsum_done, gate1_done, hot_done, load_done, counts_made, counts_read = (
            sem(n) for n in ("choice_done", "gsum_done", "gate1_done", "hot_done", "load_done", "counts_made",
                             "counts_read"))
        start_done, place_done, picked_done, placef_done, placeu_done = (
            sem(n) for n in ("start_done", "place_done", "picked_done", "placef_done", "placeu_done"))
        goal_next, goal_set, fenced, rows_sent, step_ready = (
            sem(n) for n in ("goal_next", "goal_set", "fenced", "rows_sent", "step_ready"))

        block = ctx.enter_context(nc.Block())
        x_tiles = x.rearrange("b (j p) d -> p b j d", p=P)

        @block.sync
        def _(sp):
            sp.dma_start(xall[:, 0:TILES, :], x_tiles[:, 0]).then_inc(x0_loaded, 16)
            for n, w in enumerate((Wk, Wq, Wv, Wo)):
                sp.dma_start(wraw[:, n, :], w).then_inc(w_loaded, 16)
            for n, v in enumerate((bk, bq, bv, bo)):
                sp.dma_start(rows[:, n, :], v.rearrange("(a d) -> a d", a=1)).then_inc(b_loaded, 16)
            sp.dma_start(wrraw[:], Wr).then_inc(b_loaded, 16)
            sp.dma_start(brrow[:], br.rearrange("(a d) -> a d", a=1)).then_inc(b_loaded, 16)
            for b in range(1, B):
                sp.dma_start(xall[:, TILES * b:TILES * b + TILES, :], x_tiles[:, b]).then_inc(x_loaded, 16)
            def row(v):
                return v.rearrange("(a d) -> a d", a=1)
            sp.dma_start(kept.w1raw[:], W1.rearrange("e (c p) d -> p (e c) d", p=P)).then_inc(later_loaded, 16)
            sp.dma_start(kept.w2raw[:], W2.rearrange("e p f -> p e f")).then_inc(later_loaded, 16)
            sp.dma_start(kept.b1raw[:], b1.rearrange("e (c p) -> (e c) p", p=P)).then_inc(later_loaded, 16)
            sp.dma_start(kept.rows[:, 0:D], row(gamma)).then_inc(later_loaded, 16)
            sp.dma_start(kept.rows[:, D:2 * D], row(beta)).then_inc(later_loaded, 16)
            sp.dma_start(kept.rows[:, 2 * D:], b2.rearrange("(a e) d -> a (e d)", a=1)).then_inc(later_loaded, 16)
            sp.wait_ge(later_loaded, 16 * 6)

        @block.gpsimd
        def _(pool):
            nc.gpsimd.memset(ident[:], 0.0).then_inc(ident_zero, 1)
            pool.wait_ge(ident_zero, 1)
            nc.gpsimd.affine_select(out=ident[:], in_=ident[:], compare_op=ALU.not_equal, fill=1.0, base=0,
                                    pattern=[[-1, P]], channel_multiplier=1).then_inc(ident_ready, 1)
            nc.gpsimd.memset(power[:], -0.5).then_inc(pool_consts, 1)
            nc.gpsimd.memset(eps[:], EPS).then_inc(pool_consts, 1)
            nc.gpsimd.memset(mneg[:], 0.0).then_inc(pool_consts, 1)
            nc.gpsimd.memset(vst[:], 0.0).then_inc(pool_consts, 1)
            pool.wait_ge(pool_consts, 4)
            nc.gpsimd.memset(vst[:, :, :, HD:HD + 1], 1.0).then_inc(pool_consts, 1)
            nc.gpsimd.memset(xrow[:], 0.0)
            nc.gpsimd.memset(zero[:], 0)
            nc.gpsimd.memset(step[:], S)
            nc.gpsimd.iota(goal[:].bitcast(I32), [[N, 2], [P, TILES]], base=-S, channel_multiplier=1)
            nc.gpsimd.iota(iota8[:], [[1, E]], base=0, channel_multiplier=0, allow_small_or_imprecise_dtypes=True)
            nc.gpsimd.iota(kept.origin[:], [[REGION, E]], base=0, channel_multiplier=0,
                           allow_small_or_imprecise_dtypes=True)
            nc.gpsimd.iota(fill[:], [[REGION, E]], base=0, channel_multiplier=0,
                           allow_small_or_imprecise_dtypes=True)
            nc.gpsimd.memset(ones_sq[:], 1.0).then_inc(step_ready, 1)
            pool.wait_ge(step_ready, 1)
            nc.gpsimd.affine_select(out=before[:], in_=ones_sq[:], compare_op=ALU.is_gt, fill=0.0, base=0,
                                    pattern=[[1, P]], channel_multiplier=-1).then_inc(step_ready, 1)

            def beat(t):
                if (b := t.every(GROUPS, -10, B)) is not None:
                    t.wait(pool, moments_done, b + 1, 1)
                    nc.gpsimd.tensor_tensor(vareps[:], moments[:, :, 1], eps[:], ALU.add).then_inc(vareps_done, 1)
                    t.wait(pool, vareps_done, b + 1, 1)
                    if b > 0:
                        t.wait(pool, xn_done, b, 1)
                    nc.gpsimd.tensor_tensor(rstd[:], vareps[:], power[:], ALU.pow).then_inc(rstd_done, 1)

                if (b := t.every(GROUPS, 35, B)) is not None:
                    t.wait(pool, moments2_done, b + 1, 1)
                    nc.gpsimd.tensor_tensor(vareps2[:], moments2[:, :, 1], eps[:], ALU.add).then_inc(vareps2_done, 1)
                    t.wait(pool, vareps2_done, b + 1, 1)
                    nc.gpsimd.tensor_tensor(rstd2[:], vareps2[:], power[:], ALU.pow).then_inc(rstd2_done, 1)
                if (b := t.every(GROUPS, 37, B)) is not None:
                    t.wait(pool, xn2_done, b + 1, 1)
                    nc.gpsimd.tensor_tensor(goal[:], goal[:], step[:], ALU.add).then_inc(goal_next, 1)
                    nc.gpsimd.tensor_copy(xrow[:, 1, :, 0:D], xrow[:, 0, :, 0:D])
                    nc.gpsimd.tensor_copy(kept.xn2[:, t.tiles(b), :], xrow[:, 0, :, 0:D])
                    t.wait(pool, goal_next, b + 1, 1)
                    nc.gpsimd.tensor_tensor(xrow[:, :, :, D].bitcast(U32), goal[:], zero[:], ALU.add)\
                        .then_inc(goal_set, 1)
                if (b := t.every(GROUPS, 45, B)) is not None:
                    t.wait(pool, placeu_done, b + 1, 1)
                    t.wait(pool, goal_set, b + 1, 1)
                    nc.gpsimd.tensor_tensor(fence[:], zero[:], zero[:], ALU.add)
                    for k in range(2):
                        for j in range(TILES):
                            nc.gpsimd.indirect_dma_start(
                                out=sent, out_offset=bass.IndirectOffsetOnAxis(ap=placeu[:, j, k:k + 1], axis=0),
                                in_=xrow[:, k, j, :], in_offset=None).then_inc(rows_sent, 16)

            for T in range(FIRST_BEAT, LOOP_FROM):
                beat(Beat(T))
                if T == -1:
                    pool.wait_ge(x0_loaded, 16)
                    pool.wait_ge(x_loaded, 16 * (B - 1))
                    pool.wait_ge(cols_ready, 1)
                    nc.gpsimd.tensor_tensor(
                        xres[:], xall[:], bob[:].unsqueeze(1).to_broadcast([P, B * TILES, D]), ALU.add
                    ).then_inc(xbo_done, 1)
            with pool.Fori(0, LOOPS) as turn:
                for T in range(LOOP_FROM, LOOP_FROM + GROUPS):
                    beat(Beat(T, turn))
            for T in range(LOOP_FROM + GROUPS * LOOPS, LAST_BEAT + 1):
                beat(Beat(T))
            pool.wait_ge(rows_sent, 16 * 2 * TILES * B)

        @block.scalar
        def _(act):
            act.wait_ge(consts_ready, 1)
            act.wait_ge(w_turned, 1)
            for n in range(2):
                for r in range(3):
                    nc.scalar.copy(
                        wh[:, n].rearrange("p c (g r d) -> p c g r d", g=4, d=HD)[:, :, :, r, :],
                        side_psum[:, 0, P * n:P * n + P].rearrange("p (c g d) -> p c g d", c=QUADS, d=HD))
            nc.scalar.copy(wvh[:], side_psum[:, 0, 2 * P:3 * P])
            nc.scalar.copy(woh[:], side_psum[:, 0, 3 * P:4 * P]).then_inc(w_high, 1)

            def beat(t):
                if (q := t.every(4, -4, QUADS * B)) is not None:
                    t.wait(act, side_done, SIDE["Q", q] + 1, SIDES)
                    for v in range(2):
                        nc.scalar.activation(qs[v][:, q % QUADS, :], qst[:], ACT.Copy,
                                             scale=bcol[:, 2 * QUADS + 2 + v:2 * QUADS + 3 + v]).then_inc(q_parted, 1)
                if (q := t.every(4, 11, QUADS * B)) is not None:
                    t.wait(act, pv_made, 4 * q + 4, GROUPS)
                    if q >= 2:
                        t.wait(act, o_turned, q - 1, QUADS)
                    nc.scalar.copy(pvs[:, q % 2, :], pv_psum[:, 0, :]).then_inc(pv_copied, 1)
                n = t.st()
                for g in range(4):
                    if n is not None:
                        k = 4 * n + g
                        t.wait(act, st_made, k + 1, 4 * GROUPS)
                        if n >= PT_SLOTS and g == 0:
                            t.wait(act, pv_made, n - PT_SLOTS + 1, GROUPS)
                        nc.scalar.activation(pt[:, n % PT_SLOTS, g, :], st_psum[:, st_bank(k), :], ACT.Exp,
                                             scale=SCALE).then_inc(exp_done, 1)
                    if g == 1 and side_task(t.T):
                        kind, of = side_task(t.T)
                        i = SIDE[kind, of]
                        if kind in ("K", "Q"):
                            w = 0 if kind == "K" else 1
                            c = of % QUADS
                            col = 2 * QUADS + w
                            t.wait(act, side_made, i + 1, SIDES)
                            nc.scalar.activation(hm[:], side_psum[:, 0, :], ACT.Identity,
                                                 bias=bmask[:, QUADS * w + c:QUADS * w + c + 1],
                                                 scale=bcol[:, col:col + 1]).then_inc(side_high, 1)
                        elif kind == "X2T":
                            t.wait(act, side_made, i + 1, SIDES)
                            nc.scalar.copy(xt2[:], side_psum[:, 0, :]).then_inc(side_done, 1)
                        elif kind == "XT":
                            t.wait(act, side_made, i + 1, SIDES)
                            nc.scalar.copy(xth[:], side_psum[:, 0, :]).then_inc(side_high, 1)
                        elif kind == "OT":
                            t.wait(act, side_made, i + 1, SIDES)
                            nc.scalar.copy(oth[:], side_psum[:, 0, :]).then_inc(side_high, 1)

            def beat_and_gates(t):
                beat(t)
                if (b := t.every(GROUPS, 41, B)) is not None:
                    t.wait(act, gap_done, b + 1, 1)
                    nc.scalar.activation(gexp[:], gap[:], ACT.Exp).then_inc(gexp_done, 1)

            act.wait_ge(cols_ready, 1)
            beats(act, beat_and_gates)


        high_before = {}
        for task, i in sorted(SIDE.items(), key=lambda kv: kv[1]):
            high_before[task] = sum(1 for (kind, _), j in SIDE.items() if j <= i and kind in ("K", "Q", "XT", "OT"))

        @block.vector
        def _(dve):
            nc.vector.memset(wh[:].bitcast(U32), 0)
            nc.vector.memset(wl[:].bitcast(U32), 0)
            nc.vector.memset(brow[:], 0.0)
            nc.vector.memset(mrow[:], 0.0)
            nc.vector.memset(ones[:], 1.0).then_inc(consts_ready, 1)
            dve.wait_ge(consts_ready, 1)
            dve.wait_ge(b_loaded, 96)
            for n in range(2):
                for r in range(3):
                    nc.vector.tensor_copy(
                        brow[:, n].rearrange("p c (g r d) -> p c g r d", g=4, d=HD)[:, :, :, r, :],
                        rows[:, n, :].rearrange("p (c g d) -> p c g d", c=QUADS, d=HD))
            nc.vector.memset(brow[:, 0].rearrange("p c (g r) -> p c g r", g=4)[:, :, :, SHIFT_ROW], 1.0)
            for n, r in ((0, 2), (1, 1)):
                nc.vector.memset(mrow[:, n].rearrange("p (g r) -> p g r", g=4)[:, :, HD * r:HD * r + HD], 1.0)
                nc.vector.memset(mrow[:, 2 + n].rearrange("p (g v r) -> p g v r", g=2, v=2)[:, :, n, :], 1.0)\
                    .then_inc(rows_ready, 1)
            dve.wait_ge(w_high, 1)
            for n in range(2):
                for r in range(3):
                    def stack(w):
                        return w[:, n].rearrange("p c (g r d) -> p c g r d", g=4, d=HD)[:, :, :, r, :]
                    nc.vector.tensor_tensor(
                        stack(wl), side_psum[:, 0, P * n:P * n + P].rearrange("p (c g d) -> p c g d", c=QUADS, d=HD),
                        stack(wh).bitcast(F32), ALU.subtract)
            nc.vector.tensor_tensor(wvl[:], side_psum[:, 0, 2 * P:3 * P], wvh[:].bitcast(F32), ALU.subtract)
            nc.vector.tensor_tensor(wol[:], side_psum[:, 0, 3 * P:4 * P], woh[:].bitcast(F32), ALU.subtract)\
                .then_inc(w_ready, 1)
            dve.wait_ge(cols_made, 1)
            nc.vector.tensor_copy(bcol[:], turn_psum[:, 0, 0:2 * QUADS + 4]).then_inc(setup_used, 1)
            nc.vector.tensor_copy(bvb[:], turn_psum[:, 0, 128:256])
            nc.vector.tensor_copy(bob[:], turn_psum[:, 0, 256:384])
            nc.vector.tensor_copy(brb[:], turn_psum[:, 0, 384:384 + E])
            nc.vector.tensor_copy(wrt[:], turn_psum[:, 0, 400:400 + E])
            dve.wait_ge(setup_used, 1)
            for n in range(2):
                ins = nc.vector.tensor_scalar(bmask[:, QUADS * n:QUADS * n + QUADS],
                                              bcol[:, QUADS * n:QUADS * n + QUADS],
                                              bcol[:, 2 * QUADS + n:2 * QUADS + n + 1], None, ALU.mult)
            ins.then_inc(cols_ready, 1)

            def maxima(t, g):
                n = t.scores()
                if n is None:
                    return
                k = 4 * n + g
                t.wait(dve, s_made, k + 1, 4 * GROUPS)
                if n == 0 and g == 0:
                    dve.wait_ge(pool_consts, 5)
                nc.vector.tensor_reduce(mneg[:, (n // 4) % 2, n % 4, 32 * g + SHIFT_ROW:32 * g + SHIFT_ROW + 1],
                                        s_psum[:, k % 2, :], AX_X, ALU.max, negate=True).then_inc(max_done, 1)

            def beat(t):
                if (b := t.every(GROUPS, -10, B)) is not None:
                    t.wait(dve, stats_done, b + 1, 1)
                if (b := t.every(GROUPS, 34, B)) is not None:
                    t.wait(dve, side_done, SIDE["O", b] + 1, SIDES)
                if (b := t.every(GROUPS, 35, B)) is not None:
                    t.wait(dve, stats2_done, b + 1, 1)
                if (b := t.every(GROUPS, 40, B)) is not None:
                    t.wait(dve, logits_read, b + 1, 1)
                if (b := t.every(GROUPS, 41, B)) is not None:
                    t.wait(dve, top_done, b + 1, 1)
                maxima(t, 0)
                maxima(t, 1)
                if (q := t.every(4, 4, QUADS * B)) is not None:
                    c = q % QUADS
                    t.wait(dve, shift_turned, q + 1, QUADS)
                    for v in range(2):
                        nc.vector.scalar_tensor_tensor(
                            out=qs[v][:, c, :], in0=turn_psum[:, 0, :],
                            scalar=bcol[:, 2 * QUADS + 2 + v:2 * QUADS + 3 + v],
                            in1=qs[v][:, c, :].bitcast(F32), op0=ALU.mult, op1=ALU.add).then_inc(shift_added, 1)
                if (q := t.every(4, 14, QUADS * B)) is not None:
                    c = q % QUADS
                    t.wait(dve, o_turned, q + 1, QUADS)
                    sums = turn_psum[:, 0, :].rearrange("p (j g r) -> p j g r", j=TILES, g=4)
                    nc.vector.reciprocal(rden[:], sums[:, :, :, HD]).then_inc(rden_done, 1)
                    t.wait(dve, rden_done, q + 1, QUADS)
                    nc.vector.tensor_tensor(
                        onorm[:].rearrange("p j (h d) -> p j h d", d=HD)[:, :, 4 * c:4 * c + 4, :],
                        sums[:, :, :, 0:HD], rden[:].unsqueeze(3).to_broadcast([P, TILES, 4, HD]),
                        ALU.mult).then_inc(o_normed, 1)
                maxima(t, 2)
                maxima(t, 3)
                if side_task(t.T):
                    kind, of = side_task(t.T)
                    i = SIDE[kind, of]
                    if kind in ("K", "Q"):
                        c = of % QUADS
                        w, dst = (0, kst[:, c, :]) if kind == "K" else (1, qst[:])
                        if kind == "Q" and of > 0:
                            t.wait(dve, q_parted, 2 * of, 2 * QUADS)
                        t.wait(dve, side_high, high_before[kind, of], HIGHS)
                        nc.vector.scalar_tensor_tensor(
                            out=dst, in0=side_psum[:, 0, :],
                            scalar=bcol[:, QUADS * w + c:QUADS * w + c + 1], in1=hm[:].bitcast(F32),
                            op0=ALU.add, op1=ALU.subtract).then_inc(side_done, 1)
                    elif kind in ("XT", "OT"):
                        hi, lo = (xth, xtl) if kind == "XT" else (oth, otl)
                        t.wait(dve, side_high, high_before[kind, of], HIGHS)
                        nc.vector.tensor_tensor(lo[:], side_psum[:, 0, :], hi[:].bitcast(F32), ALU.subtract)\
                            .then_inc(side_done, 1)
                    elif kind == "V":
                        c = of % QUADS
                        t.wait(dve, side_made, i + 1, SIDES)
                        if of < QUADS:
                            dve.wait_ge(pool_consts, 5)
                        nc.vector.tensor_tensor(
                            vst[:, :, 4 * c:4 * c + 4, 0:HD],
                            side_psum[:, 0, 0:P].rearrange("p (j g d) -> p j g d", j=TILES, d=HD),
                            bvb[:, 32 * c:32 * c + 32].rearrange("p (g d) -> p g d", d=HD).unsqueeze(1)
                            .to_broadcast([P, TILES, 4, HD]), ALU.add).then_inc(side_done, 1)
                    elif kind == "O":
                        t.wait(dve, side_made, i + 1, SIDES)
                        if of == 0:
                            dve.wait_ge(xbo_done, 1)
                        at = t.tiles(of)
                        nc.vector.tensor_tensor(
                            xres[:, at, :], side_psum[:, 0, :].rearrange("p (j d) -> p j d", j=TILES),
                            xres[:, at, :], ALU.add).then_inc(side_done, 1)
                if (b := t.every(GROUPS, -11, B)) is not None:
                    if b == 0:
                        dve.wait_ge(x0_loaded, 16)
                    else:
                        dve.wait_ge(x_loaded, 16 * (B - 1))
                    for j in range(TILES):
                        ins = nc.vector.bn_stats(stats[:, j, :], xall[:, t.tiles(b, j, 1), :])
                    ins.then_inc(stats_done, 1)
                if t.every(GROUPS, -10, B) is not None:
                    for j in range(TILES):
                        ins = nc.vector.bn_aggr(moments[:, j, :], stats[:, j, :])
                    ins.then_inc(moments_done, 1)
                if (b := t.every(GROUPS, -9, B)) is not None:
                    t.wait(dve, rstd_done, b + 1, 1)
                    for j in range(TILES):
                        ins = nc.vector.tensor_scalar(
                            xn[:, j:j + 1, :], xall[:, t.tiles(b, j, 1), :],
                            moments[:, j, 0:1], rstd[:, j:j + 1], ALU.subtract, ALU.mult)
                    ins.then_inc(xn_done, 1)
                route(t)

            def route(t):
                if (b := t.every(GROUPS, 34, B)) is not None:
                    for j in range(TILES):
                        ins = nc.vector.bn_stats(stats2[:, j, :], xres[:, t.tiles(b, j, 1), :])
                    ins.then_inc(stats2_done, 1)
                if t.every(GROUPS, 35, B) is not None:
                    for j in range(TILES):
                        ins = nc.vector.bn_aggr(moments2[:, j, :], stats2[:, j, :])
                    ins.then_inc(moments2_done, 1)
                if (b := t.every(GROUPS, 36, B)) is not None:
                    t.wait(dve, rstd2_done, b + 1, 1)
                    if b > 0:
                        t.wait(dve, rows_sent, 16 * 2 * TILES * b, 16 * 2 * TILES)
                    else:
                        dve.wait_ge(step_ready, 2)
                    for j in range(TILES):
                        ins = nc.vector.tensor_scalar(
                            xrow[:, 0, j:j + 1, 0:D], xres[:, t.tiles(b, j, 1), :],
                            moments2[:, j, 0:1], rstd2[:, j:j + 1], ALU.subtract, ALU.mult)
                    ins.then_inc(xn2_done, 1)
                if (b := t.every(GROUPS, 39, B)) is not None:
                    t.wait(dve, logits_made, b + 1, 1)
                    nc.vector.tensor_tensor(
                        logits[:], turn_psum[:, 0, 0:TILES * E].rearrange("p (j e) -> p j e", e=E),
                        brb[:].unsqueeze(1).to_broadcast([P, TILES, E]), ALU.add).then_inc(logits_read, 1)
                if t.every(GROUPS, 40, B) is not None:
                    for j in range(TILES):
                        ins = nc.vector.max(top[:, j, :], logits[:, j, :])
                    ins.then_inc(top_done, 1)
                if t.every(GROUPS, 41, B) is not None:
                    nc.vector.tensor_tensor(gap[:], top[:, :, 1], top[:, :, 0], ALU.subtract).then_inc(gap_done, 1)
                    for j in range(TILES):
                        ins = nc.vector.max_index(topi[:, j, :], top[:, j, :], logits[:, j, :])
                    ins.then_inc(topi_done, 1)
                if (b := t.every(GROUPS, 42, B)) is not None:
                    t.wait(dve, gexp_done, b + 1, 1)
                    nc.vector.tensor_scalar_add(gsum[:], gexp[:], 1.0).then_inc(gsum_done, 1)
                    t.wait(dve, topi_done, b + 1, 1)
                    nc.vector.tensor_copy(choice[:], topi[:, :, 0:2]).then_inc(choice_done, 1)
                    t.wait(dve, choice_done, b + 1, 1)
                    nc.vector.tensor_tensor(hot[:], iota8[:].unsqueeze(1).unsqueeze(1).to_broadcast([P, TILES, 2, E]),
                                            choice[:].unsqueeze(3).to_broadcast([P, TILES, 2, E]), ALU.is_equal)\
                        .then_inc(hot_done, 1)
                    t.wait(dve, gsum_done, b + 1, 1)
                    nc.vector.reciprocal(gsum[:], gsum[:]).then_inc(gate1_done, 1)
                    t.wait(dve, hot_done, b + 1, 1)
                    nc.vector.tensor_tensor(load[:], hot[:, :, 0, :], hot[:, :, 1, :], ALU.add).then_inc(load_done, 1)
                    t.wait(dve, gate1_done, b + 1, 1)
                    nc.vector.tensor_copy(gates[:, t.tiles(b), 0], gsum[:])
                    nc.vector.tensor_tensor(gates[:, t.tiles(b), 1], gsum[:], gexp[:], ALU.mult)
                if (b := t.every(GROUPS, 43, B)) is not None:
                    t.wait(dve, counts_made, b + 1, 1)
                    nc.vector.tensor_copy(counts[:], turn_psum[:, 0, 0:2 * TILES * E].rearrange(
                        "p (a j e) -> p a j e", a=2, e=E)).then_inc(counts_read, 1)
                if (b := t.every(GROUPS, 44, B)) is not None:
                    t.wait(dve, counts_read, b + 1, 1)
                    nc.vector.tensor_copy(start[:, 0, :], fill[:]).then_inc(start_done, 1)
                    for j in range(TILES):
                        t.wait(dve, start_done, TILES * b + j + 1 + b, TILES + 1)
                        nc.vector.tensor_tensor(start[:, j + 1, :] if j < TILES - 1 else fill[:], start[:, j, :],
                                                counts[:, 1, j, :], ALU.add).then_inc(start_done, 1)
                    t.wait(dve, start_done, (TILES + 1) * (b + 1), TILES + 1)
                    nc.vector.tensor_tensor(place[:], start[:], counts[:, 0], ALU.add).then_inc(place_done, 1)
                    t.wait(dve, place_done, b + 1, 1)
                    nc.vector.tensor_tensor(picked[:], hot[:], place[:].unsqueeze(2).to_broadcast([P, TILES, 2, E]),
                                            ALU.mult).then_inc(picked_done, 1)
                    t.wait(dve, picked_done, b + 1, 1)
                    nc.vector.tensor_reduce(placef[:], picked[:], AX_X, ALU.add).then_inc(placef_done, 1)
                    t.wait(dve, placef_done, b + 1, 1)
                    nc.vector.tensor_copy(placeu[:], placef[:]).then_inc(placeu_done, 1)

            beats(dve, beat)

        @block.tensor
        def _(pe):
            mm = nc.tensor.matmul

            def split3(dst, ah, al, bh, bl):
                mm(dst, ah, bh, start=True, stop=False)
                mm(dst, al, bh, start=False, stop=False)
                return mm(dst, ah, bl, start=False, stop=True)

            pe.wait_ge(ident_ready, 1)
            pe.wait_ge(w_loaded, 64)
            for n in range(4):
                ins = nc.tensor.transpose(side_psum[:, 0, P * n:P * n + P], wraw[:, n, :], ident[:])
            ins.then_inc(w_turned, 1)
            pe.wait_ge(rows_ready, 2)
            for n in range(2):
                for c in range(QUADS):
                    mm(turn_psum[:, 0, QUADS * n + c:QUADS * n + c + 1], brow[:, n, c, :], ones[:, 0:1],
                       start=True, stop=True)
            for n in range(4):
                mm(turn_psum[:, 0, 2 * QUADS + n:2 * QUADS + n + 1], mrow[:, n, :], ones[:, 0:1], start=True, stop=True)
            mm(turn_psum[:, 0, 384:384 + E], ones[:], brrow[:], start=True, stop=True)
            nc.tensor.transpose(turn_psum[:, 0, 400:400 + E], wrraw[:], ident[0:E, 0:E])
            for n in (2, 3):
                ins = mm(turn_psum[:, 0, 128 * (n - 1):128 * n], ones[:], rows[:, n, :], start=True, stop=True)
            ins.then_inc(cols_made, 1)
            pe.wait_ge(w_ready, 1)
            pe.wait_ge(cols_ready, 1)

            def scores(t, g):
                n = t.scores()
                if n is None:
                    return
                k, q = 4 * n + g, n // 4
                if n % 4 == 0 and g == 0:
                    t.wait(pe, q_parted, 2 * q + 2, 2 * QUADS)
                if k >= 2:
                    t.wait(pe, max_done, k - 1, 4 * GROUPS)
                r = slice(64 * (g // 2), 64 * (g // 2) + 64)
                mm(s_psum[:, k % 2, :], qs[g % 2][r, q % QUADS, P * (n % 4):P * (n % 4) + P], kst[r, q % QUADS, :],
                   start=True, stop=True).then_inc(s_made, 1)

            def scores_t(t, g):
                n = t.st()
                if n is None:
                    return
                k, q = 4 * n + g, n // 4
                if n % 4 == 0 and g == 0:
                    t.wait(pe, shift_added, 2 * q + 2, 2 * QUADS)
                if st_bank_last_user(k) >= 0:
                    t.wait(pe, exp_done, st_bank_last_user(k) + 1, 4 * GROUPS)
                r = slice(64 * (g // 2), 64 * (g // 2) + 64)
                mm(st_psum[:, st_bank(k), :], kst[r, q % QUADS, P * (n % 4):P * (n % 4) + P], qs[g % 2][r, q % QUADS, :],
                   start=True, stop=True).then_inc(st_made, 1)

            def turn(t):
                if (q := t.every(4, 4, QUADS * B)) is not None:
                    t.wait(pe, max_done, 16 * q + 16, 4 * GROUPS)
                    if q - 2 > 0:
                        t.wait(pe, o_normed, q - 2, QUADS)
                    if (b := t.every(GROUPS, 40, B)) is not None:
                        t.wait(pe, logits_read, b + 1, 1)
                    if (b := t.every(GROUPS, 44, B)) is not None:
                        t.wait(pe, counts_read, b + 1, 1)
                    for j in range(TILES):
                        ins = nc.tensor.transpose(turn_psum[:, 0, P * j:P * j + P], mneg[:, q % 2, j, :], ident[:])
                    ins.then_inc(shift_turned, 1)
                if (q := t.every(4, 14, QUADS * B)) is not None:
                    t.wait(pe, pv_copied, q + 1, QUADS)
                    if isinstance(t.turn, int) and (b := t.every(GROUPS, 42, B)) is not None:
                        t.wait(pe, logits_read, b + 1, 1)
                    if q + 3 <= QUADS * B:
                        t.wait(pe, shift_added, 2 * q + 6, 2 * QUADS)
                    else:
                        t.wait(pe, o_normed, q, QUADS)
                    for j in range(TILES):
                        ins = nc.tensor.transpose(turn_psum[:, 0, P * j:P * j + P], pvs[:, q % 2, P * j:P * j + P],
                                                  ident[:])
                    ins.then_inc(o_turned, 1)
                if (b := t.every(GROUPS, 39, B)) is not None:
                    t.wait(pe, side_done, SIDE["X2T", b] + 1, SIDES)
                    t.wait(pe, o_normed, min(QUADS * b + 7, QUADS * B), QUADS)
                    if isinstance(t.turn, int) and b > 0:
                        t.wait(pe, counts_read, b, 1)
                    for j in range(TILES):
                        ins = mm(turn_psum[:, 0, E * j:E * j + E], xt2[:, P * j:P * j + P], wrt[:],
                                 start=True, stop=True)
                    ins.then_inc(logits_made, 1)
                if (b := t.every(GROUPS, 43, B)) is not None:
                    t.wait(pe, load_done, b + 1, 1)
                    t.wait(pe, o_normed, min(QUADS * b + 8, QUADS * B), QUADS)
                    flat = load[:].rearrange("p j e -> p (j e)")
                    mm(turn_psum[:, 0, 0:TILES * E], before[:], flat, start=True, stop=True)
                    mm(turn_psum[:, 0, TILES * E:2 * TILES * E], ones_sq[:], flat, start=True, stop=True)\
                        .then_inc(counts_made, 1)

            def side(t):
                if not side_task(t.T):
                    return
                kind, of = side_task(t.T)
                i = SIDE[kind, of]
                t.wait(pe, side_done, i, SIDES)
                c = of % QUADS
                if kind == "XT":
                    t.wait(pe, xn_done, of + 1, 1)
                    for j in range(TILES):
                        ins = nc.tensor.transpose(side_psum[:, 0, P * j:P * j + P], xn[:, j, :], ident[:])
                elif kind in ("K", "Q"):
                    w = 0 if kind == "K" else 1
                    ins = split3(side_psum[:, 0, :], wh[:, w, c, :], wl[:, w, c, :], xth[:], xtl[:])
                elif kind == "X2T":
                    t.wait(pe, xn2_done, of + 1, 1)
                    for j in range(TILES):
                        ins = nc.tensor.transpose(side_psum[:, 0, P * j:P * j + P], xrow[:, 0, j, 0:D], ident[:])
                elif kind == "V":
                    for j in range(TILES):
                        ins = split3(side_psum[:, 0, 32 * j:32 * j + 32], xth[:, P * j:P * j + P],
                                     xtl[:, P * j:P * j + P], wvh[:, 32 * c:32 * c + 32], wvl[:, 32 * c:32 * c + 32])
                elif kind == "OT":
                    t.wait(pe, o_normed, QUADS * (of + 1), QUADS)
                    for j in range(TILES):
                        ins = nc.tensor.transpose(side_psum[:, 0, P * j:P * j + P], onorm[:, j, :], ident[:])
                else:
                    for j in range(TILES):
                        ins = split3(side_psum[:, 0, P * j:P * j + P], oth[:, P * j:P * j + P],
                                     otl[:, P * j:P * j + P], woh[:], wol[:])
                ins.then_inc(side_made, 1)

            def values(t):
                n = t.pv()
                if n is None:
                    return
                q = n // 4
                t.wait(pe, exp_done, 4 * n + 4, 4 * GROUPS)
                if n % 4 == 0:
                    t.wait(pe, side_done, SIDE["V", q] + 1, SIDES)
                    if q > 0:
                        t.wait(pe, pv_copied, q, QUADS)
                for g in range(4):
                    ins = mm(pv_psum[32 * g:32 * g + 32, 0, :], vst[:, n % 4, 4 * (q % QUADS) + g, :],
                             pt[:, n % PT_SLOTS, g, :], start=(n % 4 == 0), stop=(n % 4 == 3))
                ins.then_inc(pv_made, 1)

            def beat(t):
                scores(t, 0)
                scores(t, 1)
                turn(t)
                scores_t(t, 0)
                scores_t(t, 1)
                side(t)
                scores(t, 2)
                scores(t, 3)
                scores_t(t, 2)
                scores_t(t, 3)
                values(t)

            beats(pe, beat)


def experts(nc, kept, sent, results, out):
    with ExitStack() as ctx:
        def sb(name, shape, dt=F32):
            return ctx.enter_context(nc.sbuf_tensor(name, shape, dt))

        def sem(name):
            return ctx.enter_context(nc.semaphore(name))

        def psum(name, banks=1):
            return ctx.enter_context(nc.psum_tensor(name, [P, banks, 512], F32))

        ident, w1raw, w2raw, b1raw, rows = kept.ident, kept.w1raw, kept.w2raw, kept.b1raw, kept.rows
        w1h = sb("w1h", [P, E * FC, P], F32R)
        w1l = sb("w1l", [P, E * FC, P], F32R)
        w2t = sb("w2t", [P, E * FC, D])
        b1c = sb("b1c", [P, E * FC])
        spread = sb("spread", [P, (2 + E) * D])
        ones_row = sb("ones_row", [1, P])
        tokens = sb("tokens", [P, E])
        tokens_i = sb("tokens_i", [P, E], I32)
        turns_i = sb("turns_i", [P, E], I32)
        turns_f = sb("turns_f", [P, E])
        sums_f = sb("sums_f", [P, E])
        no_turns = sb("no_turns", [P, E])
        table = sb("table", [P, 3 * E], I32)
        tail = sb("tail", [P, HALVES, ROW])
        eps2, power2 = sb("eps2", [P, TILES]), sb("power2", [P, TILES])
        lot = sb("lot", [P, HALVES, ROW])
        xh, xl = sb("xh", [P, SLOTS], F32R), sb("xl", [P, SLOTS], F32R)
        hid = sb("hid", [P, FC, SLOTS])
        res = sb("res", [P, HALVES, D])
        goal_now = sb("goal_now", [P, HALVES], U32)
        goal_new = sb("goal_new", [P, HALVES], U32)
        zero2 = sb("zero2", [P, HALVES], U32)
        fence2 = sb("fence2", [P, HALVES], U32)
        got = sb("got", [P, 2, TILES * B, D])
        z = sb("z", [P, 2, TILES, D])
        stats3 = sb("stats3", [P, TILES, 6])
        moments3 = sb("moments3", [P, 2, TILES, 2])
        vareps3, rstd3 = sb("vareps3", [P, TILES]), sb("rstd3", [P, 2, TILES])
        fin = sb("fin", [P, 2, TILES, D])

        h_psum = psum("h_psum", FC)
        y_psum = psum("y_psum")
        x_psum = psum("x_psum")
        w_psum = psum("w_psum", 2)

        const_ready, turned, high, low, small_made, small_done = (
            sem(n) for n in ("const_ready", "turned", "high", "low", "small_made", "small_done"))
        chain, table_ready, ones_ready = sem("chain"), sem("table_ready"), sem("ones_ready")
        rows_stored, lot_loaded, lot_turned, goals_taken, goals_now = (
            sem(n) for n in ("rows_stored", "lot_loaded", "lot_turned", "goals_taken", "goals_now"))
        xh_done, xl_done, h_made, relu_act, relu_dve, y_made, y_done = (
            sem(n) for n in ("xh_done", "xl_done", "h_made", "relu_act", "relu_dve", "y_made", "y_done"))
        got_in, z1, z_done, s3_done, m3_done, v3_done, r3_done = (
            sem(n) for n in ("got_in", "z1", "z_done", "s3_done", "m3_done", "v3_done", "r3_done"))
        n_done, g_done, beta_added, fin_done, stored, xpart = (
            sem(n) for n in ("n_done", "g_done", "beta_added", "fin_done", "stored", "xpart"))

        block = ctx.enter_context(nc.Block())

        def counts_of(eng):
            eng.wait_ge(table_ready, 1)
            turns = [eng.value_load(table[0:1, e:e + 1], min_val=1, max_val=N // SLOTS) for e in range(E)]
            first = [eng.value_load(table[0:1, E + e:E + e + 1], min_val=0, max_val=LOTS) for e in range(E)]
            return turns, first

        LOTS = 2 * N // SLOTS + E
        sent_e = sent.rearrange("(e r) c -> e r c", e=E)

        @block.sync
        def _(sp):
            turns, first = counts_of(sp)
            sp.wait_ge(rows_stored, 16 * E)

            def load(src):
                sp.dma_start(lot[:], src.rearrange("(h p) c -> p h c", p=P)).then_inc(lot_loaded, 16)

            for e in range(E):
                with sp.Fori(0, turns[e]) as i:
                    at = sp.snap(i * SLOTS, min_val=0, max_val=N - SLOTS)
                    u = sp.snap(first[e] + i + 1, min_val=1, max_val=LOTS)
                    sp.wait_ge(lot_turned, u)
                    sp.wait_ge(goals_taken, u)
                    load(sent_e[e, ds(at, SLOTS), :])
            total = first[E - 1] + turns[E - 1]
            sp.wait_ge(lot_turned, total + 1)
            sp.wait_ge(goals_taken, total + 1)
            load(sent_e[0, 0:SLOTS, :])
            got_from = results.rearrange("(k t p) d -> p k t d", k=2, p=P)

            def fetch(at):
                for k in range(2):
                    sp.dma_start(got[:, k, at, :], got_from[:, k, at, :]).then_inc(got_in, 16)

            sp.wait_ge(rows_stored, total * (16 * HALVES) + 16 * E)
            fetch(slice(0, TILES))
            with sp.Fori(1, B) as b:
                at = sp.snap(b * TILES, min_val=TILES, max_val=(B - 1) * TILES)
                sp.wait_ge(got_in, b * 32)
                fetch(ds(at, TILES))

        @block.gpsimd
        def _(pool):
            nc.gpsimd.memset(eps2[:], EPS)
            nc.gpsimd.memset(power2[:], -0.5)
            nc.gpsimd.memset(no_turns[:], 0.0)
            nc.gpsimd.memset(zero2[:], 0).then_inc(goals_taken, 1)
            nc.gpsimd.memset(tail[:], 0.0).then_inc(const_ready, 1)
            pool.wait_ge(const_ready, 1)
            nc.gpsimd.memset(tail[:, :, D].bitcast(U32), NOWHERE).then_inc(const_ready, 1)
            turns, first = counts_of(pool)
            pool.wait_ge(const_ready, 2)
            for e in range(E):
                free = pool.value_load(table[0:1, 2 * E + e:2 * E + e + 1], min_val=e * REGION,
                                       max_val=e * REGION + N)
                pool.dma_start(sent[ds(free, SLOTS), :].rearrange("(h p) c -> p h c", p=P), tail[:])\
                    .then_inc(rows_stored, 16)
            pool.wait_ge(lot_loaded, 16)
            nc.gpsimd.tensor_tensor(goal_new[:], lot[:, :, D].bitcast(U32), zero2[:], ALU.add)\
                .then_inc(goals_taken, 1)
            for e in range(E):
                with pool.Fori(0, turns[e]) as i:
                    u = first[e] + i
                    pool.wait_ge(rows_stored, u * (16 * HALVES) + 16 * E)
                    pool.wait_ge(goals_taken, u + 2)
                    nc.gpsimd.tensor_tensor(goal_now[:], goal_new[:], zero2[:], ALU.add).then_inc(goals_now, 1)
                    pool.wait_ge(lot_loaded, u * 16 + 32)
                    pool.wait_ge(goals_now, u + 1)
                    nc.gpsimd.tensor_tensor(goal_new[:], lot[:, :, D].bitcast(U32), zero2[:], ALU.add)\
                        .then_inc(goals_taken, 1)
                    pool.wait_ge(y_done, u + 2)
                    nc.gpsimd.tensor_tensor(fence2[:], zero2[:], zero2[:], ALU.add)
                    for h in range(HALVES):
                        nc.gpsimd.indirect_dma_start(
                            out=results, out_offset=bass.IndirectOffsetOnAxis(ap=goal_now[:, h:h + 1], axis=0),
                            in_=res[:, h, :], in_offset=None, bounds_check=2 * N - 1, oob_is_err=False)\
                            .then_inc(rows_stored, 16)
            with pool.Fori(0, B) as b:
                pool.wait_ge(m3_done, b + 1)
                nc.gpsimd.tensor_tensor(vareps3[:], moments3[:, 0, :, 1], eps2[:], ALU.add).then_inc(v3_done, 1)
                pool.wait_ge(v3_done, b + 1)
                nc.gpsimd.tensor_tensor(rstd3[:, 0], vareps3[:], power2[:], ALU.pow).then_inc(r3_done, 1)

        @block.scalar
        def _(act):
            for n in range(2 * E):
                act.wait_ge(turned, n + 1)
                src = w_psum[:, n % 2].rearrange("p (c d) -> p c d", c=FC)
                if n < E:
                    nc.scalar.copy(w1h[:, FC * n:FC * n + FC, :], src).then_inc(high, 1)
                else:
                    nc.scalar.copy(w2t[:, FC * (n - E):FC * (n - E) + FC, :], src).then_inc(high, 1)
            turns, first = counts_of(act)
            act.wait_ge(small_done, 1)

            def split_high(count):
                act.wait_ge(lot_turned, count)
                nc.scalar.copy(xh[:], x_psum[:, 0, 0:SLOTS]).then_inc(xh_done, 1)

            split_high(2)
            for e in range(E):
                with act.Fori(0, turns[e]) as i:
                    u = first[e] + i
                    for f in range(FC - 1):
                        act.wait_ge(h_made, u * FC + f + 1)
                        nc.scalar.activation(hid[:, f, :], h_psum[:, f, 0:SLOTS], ACT.Relu,
                                             bias=b1c[:, FC * e + f:FC * e + f + 1]).then_inc(relu_act, 1)
                    split_high(u + 3)
            out_tiles = out.rearrange("b (j p) d -> p b j d", p=P)
            with act.Fori(0, B) as b:
                act.wait_ge(fin_done, b + 1)
                act.dma_start(out_tiles[:, ds(b, 1)], got[:, 0:1, ds(b * TILES, TILES), :]).then_inc(stored, 16)
            act.wait_ge(stored, 16 * B)

        @block.vector
        def _(dve):
            steps = [0]

            def link(ins):
                steps[0] += 1
                ins.then_inc(chain, 1)
                dve.wait_ge(chain, steps[0])

            nc.vector.memset(ones_row[:], 1.0).then_inc(ones_ready, 1)
            link(nc.vector.tensor_tensor(tokens[:], kept.fill[:], kept.origin[:], ALU.subtract))
            link(nc.vector.tensor_scalar_add(tokens[:], tokens[:], float(SLOTS - 1)))
            link(nc.vector.tensor_copy(tokens_i[:], tokens[:]))
            link(nc.vector.tensor_scalar(turns_i[:], tokens_i[:], SLOTS.bit_length() - 1, None,
                                         ALU.arith_shift_right))
            link(nc.vector.tensor_copy(turns_f[:], turns_i[:]))
            link(nc.vector.tensor_scalar(turns_f[:], turns_f[:], 1.0, None, ALU.max))
            dve.wait_ge(const_ready, 1)
            link(nc.vector.tensor_tensor_scan(sums_f[:], turns_f[:], no_turns[:], 0.0, ALU.add, ALU.add))
            link(nc.vector.tensor_tensor(sums_f[:], sums_f[:], turns_f[:], ALU.subtract))
            nc.vector.tensor_copy(table[:, 0:E], turns_f[:])
            nc.vector.tensor_copy(table[:, E:2 * E], sums_f[:])
            nc.vector.tensor_copy(table[:, 2 * E:3 * E], kept.fill[:]).then_inc(table_ready, 1)
            for n in range(E):
                dve.wait_ge(high, n + 1)
                nc.vector.tensor_tensor(w1l[:, FC * n:FC * n + FC, :],
                                        w_psum[:, n % 2].rearrange("p (c d) -> p c d", c=FC),
                                        w1h[:, FC * n:FC * n + FC, :].bitcast(F32), ALU.subtract).then_inc(low, 1)
            dve.wait_ge(small_made, 1)
            nc.vector.tensor_copy(b1c[:], x_psum[:, 0, 0:E * FC])
            for n in range(3):
                w = min(512, (2 + E) * D - 512 * n)
                ins = nc.vector.tensor_copy(spread[:, 512 * n:512 * n + w], h_psum[:, n, 0:w])
            ins.then_inc(small_done, 1)
            dve.wait_ge(small_done, 1)
            nc.vector.memset(fin[:, 0, 0, 0:1], 0.0).then_inc(y_done, 1)
            turns, first = counts_of(dve)

            def split_low(count):
                dve.wait_ge(xh_done, count)
                nc.vector.tensor_tensor(xl[:], x_psum[:, 0, 0:SLOTS], xh[:].bitcast(F32), ALU.subtract)\
                    .then_inc(xl_done, 1)

            split_low(1)
            for e in range(E):
                with dve.Fori(0, turns[e]) as i:
                    u = first[e] + i
                    f = FC - 1
                    dve.wait_ge(h_made, u * FC + FC)
                    nc.vector.tensor_scalar(hid[:, f, :], h_psum[:, f, 0:SLOTS],
                                            b1c[:, FC * e + f:FC * e + f + 1], 0.0, ALU.add, ALU.max)\
                        .then_inc(relu_dve, 1)
                    split_low(u + 2)
                    dve.wait_ge(y_made, u + 1)
                    dve.wait_ge(rows_stored, u * (16 * HALVES) + 16 * E)
                    nc.vector.tensor_tensor(
                        res[:], y_psum[:, 0, 0:SLOTS].rearrange("p (h d) -> p h d", h=HALVES),
                        spread[:, (2 + e) * D:(3 + e) * D].unsqueeze(1).to_broadcast([P, HALVES, D]),
                        ALU.add).then_inc(y_done, 1)

            gamma = spread[:, 0:D].unsqueeze(1).to_broadcast([P, TILES, D])
            beta = spread[:, D:2 * D].unsqueeze(1).to_broadcast([P, TILES, D])
            with dve.Fori(0, B) as b:
                dve.wait_ge(got_in, b * 32 + 32)
                for j in range(TILES):
                    at = ds(b * TILES + j, 1)
                    ins = nc.vector.scalar_tensor_tensor(
                        out=z[:, 0, j:j + 1, :], in0=got[:, 0, at, :], scalar=kept.gates[:, at, 0],
                        in1=kept.xn2[:, at, :], op0=ALU.mult, op1=ALU.add)
                ins.then_inc(z1, 1)
                dve.wait_ge(z1, b + 1)
                for j in range(TILES):
                    at = ds(b * TILES + j, 1)
                    ins = nc.vector.scalar_tensor_tensor(
                        out=z[:, 1, j:j + 1, :], in0=got[:, 1, at, :], scalar=kept.gates[:, at, 1],
                        in1=z[:, 0, j:j + 1, :], op0=ALU.mult, op1=ALU.add)
                ins.then_inc(z_done, 1)
                dve.wait_ge(z_done, b + 1)
                for j in range(TILES):
                    ins = nc.vector.bn_stats(stats3[:, j, :], z[:, 1, j, :])
                ins.then_inc(s3_done, 1)
                dve.wait_ge(s3_done, b + 1)
                nc.vector.tensor_tensor(fin[:, 1], kept.xres[:, ds(b * TILES, TILES), :], beta, ALU.add)\
                    .then_inc(xpart, 1)
                for j in range(TILES):
                    ins = nc.vector.bn_aggr(moments3[:, 0, j, :], stats3[:, j, :])
                ins.then_inc(m3_done, 1)
                dve.wait_ge(r3_done, b + 1)
                for j in range(TILES):
                    ins = nc.vector.tensor_scalar(z[:, 0, j, :], z[:, 1, j, :], moments3[:, 0, j, 0:1],
                                                  rstd3[:, 0, j:j + 1], ALU.subtract, ALU.mult)
                ins.then_inc(n_done, 1)
                dve.wait_ge(n_done, b + 1)
                nc.vector.tensor_tensor(z[:, 1], z[:, 0], gamma, ALU.mult).then_inc(g_done, 1)
                dve.wait_ge(g_done, b + 1)
                dve.wait_ge(xpart, b + 1)
                nc.vector.tensor_tensor(got[:, 0, ds(b * TILES, TILES), :], z[:, 1], fin[:, 1], ALU.add)\
                    .then_inc(fin_done, 1)

        @block.tensor
        def _(pe):
            mm = nc.tensor.matmul
            for n in range(2 * E):
                if n >= 2:
                    pe.wait_ge(high, n - 1)
                    pe.wait_ge(low, min(n - 1, E))
                for c in range(FC):
                    src = w1raw[:, FC * n + c, :] if n < E else w2raw[:, n - E, P * c:P * c + P]
                    ins = nc.tensor.transpose(w_psum[:, n % 2, P * c:P * c + P], src, ident[:])
                ins.then_inc(turned, 1)
            nc.tensor.transpose(x_psum[:, 0, 0:E * FC], b1raw[:], ident[0:E * FC, 0:E * FC])
            pe.wait_ge(ones_ready, 1)
            for n in range(3):
                w = min(512, (2 + E) * D - 512 * n)
                ins = mm(h_psum[:, n, 0:w], ones_row[:], rows[:, 512 * n:512 * n + w], start=True, stop=True)
            ins.then_inc(small_made, 1)
            turns, first = counts_of(pe)
            pe.wait_ge(high, 2 * E)
            pe.wait_ge(low, E)
            pe.wait_ge(small_done, 1)
            nc.tensor.transpose(w_psum[:, 0, 0:P], w1raw[:, 0, :], ident[:]).then_inc(lot_turned, 1)

            def turn_lot(count):
                pe.wait_ge(lot_loaded, count)
                for h in range(HALVES):
                    ins = nc.tensor.transpose(x_psum[:, 0, P * h:P * h + P], lot[:, h, 0:D], ident[:])
                ins.then_inc(lot_turned, 1)

            turn_lot(16)
            for e in range(E):
                with pe.Fori(0, turns[e]) as i:
                    u = first[e] + i
                    pe.wait_ge(xh_done, u + 1)
                    pe.wait_ge(xl_done, u + 1)
                    for f in range(FC):
                        k = FC * e + f
                        dst = h_psum[:, f, 0:SLOTS]
                        mm(dst, w1h[:, k, :], xh[:], start=True, stop=False)
                        mm(dst, w1h[:, k, :], xl[:], start=False, stop=False)
                        mm(dst, w1l[:, k, :], xh[:], start=False, stop=True).then_inc(h_made, 1)
                    turn_lot(u * 16 + 32)
                    pe.wait_ge(relu_act, u * (FC - 1) + (FC - 1))
                    pe.wait_ge(relu_dve, u + 1)
                    pe.wait_ge(y_done, u + 1)
                    for h in range(HALVES):
                        for f in range(FC):
                            ins = mm(y_psum[:, 0, P * h:P * h + P], hid[:, f, P * h:P * h + P], w2t[:, FC * e + f, :],
                                     start=(f == 0), stop=(f == FC - 1))
                    ins.then_inc(y_made, 1)


_INS = ["L0_attn_x", "L0_attn_Wq", "L0_attn_bq", "L0_attn_Wk", "L0_attn_bk", "L0_attn_Wv", "L0_attn_bv",
        "L0_attn_Wo", "L0_attn_bo", "L0_ffn_Wr", "L0_ffn_br", "L0_ffn_W1", "L0_ffn_b1", "L0_ffn_W2",
        "L0_ffn_b2", "L0_ffn_gamma", "L0_ffn_beta"]


def kernel(**inputs):
    import numpy as _np
    import concourse.bacc as _bacc
    from concourse import mybir as _mybir
    from concourse.bass_utils import run_bass_kernel_spmd as _run

    nc = _bacc.Bacc("TRN2", target_bir_lowering=False, num_devices=1)
    arrays, args = {}, []
    for name in _INS:
        a = _np.ascontiguousarray(inputs[name])
        arrays[f"in_{name}_dram"] = a
        args.append(nc.dram_tensor(f"in_{name}_dram", a.shape, _mybir.dt.from_np(a.dtype), kind="ExternalInput").ap())
    args.append(nc.dram_tensor("out_0_dram", (B, S, D), _mybir.dt.float32, kind="ExternalOutput").ap())
    layer(nc, *args)
    r = _run(nc, [arrays], core_ids=[0])
    return r.results[0]["out_0_dram"]
```

```python
from contextlib import ExitStack

import numpy as np

import concourse.bass as bass
from concourse import mybir

ALU = mybir.AluOpType
ACT = mybir.ActivationFunctionType
F32 = mybir.dt.float32
F32R = mybir.dt.float32r
U32 = mybir.dt.uint32
I32 = mybir.dt.int32
AX_X = mybir.AxisListType.X
ds = bass.ds

P = 128
B, S, D = 8, 512, 128
H = 16
HD = D // H
TILES = S // P
QUADS = H // 4
GROUPS = QUADS * TILES
E = 8
F = 512
FC = F // P
N = B * S
HALVES = 2
SLOTS = HALVES * P
REGION = N + SLOTS
GOALS = 4
TAILS = E // HALVES
ROW = D + 4
NOWHERE = 1 << 20
SCALE = float(np.float32(1.0) / np.sqrt(np.float32(HD)))
EPS = 1e-5

SCORE_ROWS = 3 * HD
SHIFT_ROW = SCORE_ROWS
ST_LAG = 5
PV_LAG = 7
FIRST_BEAT = -11
LAST_BEAT = GROUPS * (B - 1) + 46
LOOP_FROM = 37
LOOPS = 5
SIDES = 14
HIGHS = 10
PLACE_STEPS = 1 + TILES + 5
S_BANKS = 3
ST_BANKS = 2
PT_SLOTS = 4


def s_bank(k):
    k %= 4 * GROUPS
    return 1 if k == 4 * GROUPS - 1 else k % S_BANKS


def s_bank_last_user(k):
    j = k - 1
    while s_bank(j) != s_bank(k):
        j -= 1
    return j


def side_task(T):
    if T % 8 == 0:
        kind, of, n = "V", T // 8, QUADS * B // 2
    elif T % 4 == 2:
        kind, of, n = "K", (T + 6) // 4, QUADS * B
    elif T % 4 == 3:
        kind, of, n = "Q", (T + 5) // 4, QUADS * B
    elif T % GROUPS == 9:
        kind, of, n = "XT", (T + 7) // GROUPS, B
    elif T % GROUPS == 13:
        kind, of, n = "OT", (T - 29) // GROUPS, B
    elif T % GROUPS == 1:
        kind, of, n = "O", (T - 33) // GROUPS, B
    elif T % GROUPS == 5:
        kind, of, n = "X2T", (T - 37) // GROUPS, B
    else:
        return None
    return (kind, of) if 0 <= of < n else None


SIDE = {}
for _T in range(FIRST_BEAT, LAST_BEAT + 1):
    if side_task(_T):
        SIDE[side_task(_T)] = len(SIDE)


class Beat:

    def __init__(self, T, turn=0):
        self.T, self.turn = T, turn

    def scores(self):
        return self.T if 0 <= self.T < GROUPS * B else None

    def st(self):
        n = self.T - ST_LAG
        return n if 0 <= n < GROUPS * B else None

    def pv(self):
        n = self.T - PV_LAG
        return n if 0 <= n < GROUPS * B else None

    def tiles(self, b, j=0, count=TILES):
        at = TILES * b + j
        return slice(at, at + count) if isinstance(self.turn, int) else ds(self.turn * TILES + at, count)

    def every(self, period, offset, count):
        n, r = divmod(self.T - offset, period)
        return n if r == 0 and 0 <= n < count else None

    def wait(self, eng, sem, count, per_batch):
        if isinstance(self.turn, int):
            if count > 0:
                eng.wait_ge(sem, count)
        else:
            eng.wait_ge(sem, self.turn * per_batch + count)


def expert_weights(t):
    if not isinstance(t.turn, int):
        return ()
    if -E <= t.T < 0:
        return (t.T + E,)
    if 0 <= t.T < E // 2:
        return (E + 2 * t.T, E + 2 * t.T + 1)
    return ()


def beats(eng, body):
    for T in range(FIRST_BEAT, LOOP_FROM):
        body(Beat(T))
    with eng.Fori(0, LOOPS) as turn:
        for T in range(LOOP_FROM, LOOP_FROM + GROUPS):
            body(Beat(T, turn))
    for T in range(LOOP_FROM + GROUPS * LOOPS, LAST_BEAT + 1):
        body(Beat(T))


def tiles(b, j=0, count=TILES):
    return slice(b * TILES + j, b * TILES + j + count) if isinstance(b, int) else ds(b * TILES + j, count)


def layer(nc, x, Wq, bq, Wk, bk, Wv, bv, Wo, bo, Wr, br, W1, b1, W2, b2, gamma, beta, out):
    sent = nc.dram_tensor("sent", (E * REGION, ROW), F32, kind="Internal").ap()
    results = nc.dram_tensor("results", (2 * N, D), F32, kind="Internal").ap()
    unread = nc.dram_tensor("unread", (HALVES, TILES), F32, kind="Internal").ap()
    with ExitStack() as ctx:
        def sb(name, shape, dt=F32):
            return ctx.enter_context(nc.sbuf_tensor(name, shape, dt))

        kept = Kept(
            xres=sb("xres", [P, B * TILES, D]),
            xn2=sb("xn2", [P, B * TILES, D]),
            ident=sb("ident", [P, P]),
            fill=sb("fill", [P, E]),
            w1h=sb("w1h", [P, E * FC, P], F32R),
            w1l=sb("w1l", [P, E * FC, P], F32R),
            w2t=sb("w2t", [P, E * FC, D]),
            b1c=sb("b1c", [P, E * FC]),
            beta=sb("beta", [P, D]),
            table=sb("table", [P, 2 * E], I32))
        attention(nc, x, Wq, bq, Wk, bk, Wv, bv, Wo, bo, Wr, br, W1, b1, W2, beta, kept, sent)
        experts(nc, gamma, b2, kept, sent, results, unread, out)


class Kept:

    def __init__(self, xres, xn2, ident, fill, w1h, w1l, w2t, b1c, beta, table):
        self.xres, self.xn2, self.ident, self.fill = xres, xn2, ident, fill
        self.w1h, self.w1l, self.w2t, self.b1c, self.beta, self.table = w1h, w1l, w2t, b1c, beta, table
        self.turns = {}

    def count_turns(self, name, eng, table_ready):
        eng.wait_ge(table_ready, 1)
        self.turns[name] = [eng.value_load(self.table[0:1, e:e + 1], min_val=1, max_val=N // SLOTS)
                            for e in range(E)]


def attention(nc, x, Wq, bq, Wk, bk, Wv, bv, Wo, bo, Wr, br, W1, b1, W2, beta, kept, sent):
    xres, ident, fill = kept.xres, kept.ident, kept.fill
    with ExitStack() as ctx:
        def sb(name, shape, dt=F32):
            return ctx.enter_context(nc.sbuf_tensor(name, shape, dt))

        def sem(name):
            return ctx.enter_context(nc.semaphore(name))

        def psum(name, banks=1):
            return ctx.enter_context(nc.psum_tensor(name, [P, banks, 512], F32))

        qs = sb("qs", [P, QUADS, S], F32R)
        kst = sb("kst", [P, S], F32R)
        ks = sb("ks", [P, 4, QUADS, S], F32R)
        vst = sb("vst", [P, TILES, H, 32])
        pt = sb("pt", [P, PT_SLOTS, 4, S])
        pvs = sb("pvs", [P, 2, S])
        onorm = sb("onorm", [P, TILES, D])
        rden = sb("rden", [P, TILES, 4])
        mneg = sb("mneg", [P, 2, TILES, P])
        xn = sb("xn", [P, TILES, D])
        xth, xtl = sb("xth", [P, S], F32R), sb("xtl", [P, S], F32R)
        oth, otl = sb("oth", [P, S], F32R), sb("otl", [P, S], F32R)
        hm = sb("hm", [P, S], F32R)
        stats = sb("stats", [P, TILES, 6])
        moments = sb("moments", [P, TILES, 2])
        vareps = sb("vareps", [P, TILES])
        rstd = sb("rstd", [P, TILES])
        power = sb("power", [P, TILES])
        eps = sb("eps", [P, TILES])
        zero4, minus_mean, shift = sb("zero4", [P, TILES]), sb("minus_mean", [P, TILES]), sb("shift", [P, TILES])
        minus_mean2, shift2 = sb("minus_mean2", [P, TILES]), sb("shift2", [P, TILES])
        wraw = kept.xn2[:, 0:4, :]
        wh = sb("wh", [P, 2, QUADS, P], F32R)
        wl = sb("wl", [P, 2, QUADS, P], F32R)
        wvh, wvl = sb("wvh", [P, D], F32R), sb("wvl", [P, D], F32R)
        woh, wol = sb("woh", [P, D], F32R), sb("wol", [P, D], F32R)
        rows = kept.xn2[0:1, 4:8, :]
        brrow = sb("brrow", [1, E])
        brow = kept.xn2[0:1, 8:16, :].rearrange("p (n c) d -> p n c d", n=2)
        mrow = kept.xn2[0:1, 16:18, :]
        ones = sb("ones", [1, P])
        bcol = sb("bcol", [P, 2 * QUADS + 2])
        bmask = sb("bmask", [P, 2 * QUADS])
        bvb = sb("bvb", [P, D])
        brb = sb("brb", [P, E])
        wrraw = kept.xn2[0:E, 19, :]
        wrt = sb("wrt", [P, E])
        xt2 = sb("xt2", [P, S])
        xrow = sb("xrow", [P, 2, TILES, ROW])
        stats2 = sb("stats2", [P, TILES, 6])
        moments2 = sb("moments2", [P, TILES, 2])
        vareps2, rstd2 = sb("vareps2", [P, TILES]), sb("rstd2", [P, TILES])
        logits = sb("logits", [P, TILES, E])
        top = sb("top", [P, TILES, 8])
        topi = sb("topi", [P, TILES, 8], U32)
        choice = sb("choice", [P, TILES, 2])
        gap, gexp, gsum = sb("gap", [P, TILES]), sb("gexp", [P, TILES]), sb("gsum", [P, TILES])
        iota8 = sb("iota8", [P, E])
        hot = sb("hot", [P, TILES, 2, E])
        load = sb("load", [P, TILES, E])
        before = sb("before", [P, P])
        ones_sq = sb("ones_sq", [P, P])
        counts = sb("counts", [P, 2, TILES, E])
        start = sb("start", [P, TILES, E])
        place = sb("place", [P, TILES, E])
        picked = sb("picked", [P, TILES, 2, E])
        zero_e = sb("zero_e", [P, E])
        placef = sb("placef", [P, TILES, 2])
        placeu = sb("placeu", [P, TILES, 2], U32)
        goal = sb("goal", [P, 2, TILES], U32)
        step = sb("step", [P, 2, TILES], U32)
        zero = sb("zero", [P, 2, TILES], U32)
        fence = sb("fence", [P, 2, TILES], U32)
        bob = sb("bob", [P, D])
        b1raw = kept.xn2[0:E * FC, 18, :]
        w1raw = pt[:, 0:2].rearrange("p a g (c d) -> p (a g c) d", d=D)
        w2raw = pt[:, 2:4].rearrange("p a g f -> p (a g) f")
        origin = sb("origin", [P, E])
        tokens = sb("tokens", [P, E])
        tokens_i = sb("tokens_i", [P, E], I32)
        tail = sb("tail", [P, HALVES, ROW])

        s_psum = psum("s_psum", S_BANKS)
        st_psum = psum("st_psum", ST_BANKS)
        pv_psum = psum("pv_psum")
        turn_psum = psum("turn_psum")
        side_psum = psum("side_psum")

        w_loaded, b_loaded, x0_loaded, x_loaded = (sem(n) for n in ("w_loaded", "b_loaded", "x0_loaded", "x_loaded"))
        ident_zero, ident_ready, consts_ready, pool_consts = (
            sem(n) for n in ("ident_zero", "ident_ready", "consts_ready", "pool_consts"))
        rows_ready, w_turned, w_high, w_ready = (sem(n) for n in ("rows_ready", "w_turned", "w_high", "w_ready"))
        cols_made, cols_ready, setup_used = (sem(n) for n in ("cols_made", "cols_ready", "setup_used"))
        stats_done, moments_done, vareps_done, rstd_done, xn_done = (
            sem(n) for n in ("stats_done", "moments_done", "vareps_done", "rstd_done", "xn_done"))
        s_made, max_done, shift_turned, shift_added = (
            sem(n) for n in ("s_made", "max_done", "shift_turned", "shift_added"))
        st_made, exp_done, pv_made, pv_copied = (sem(n) for n in ("st_made", "exp_done", "pv_made", "pv_copied"))
        o_turned, rden_done, o_normed = (sem(n) for n in ("o_turned", "rden_done", "o_normed"))
        side_made, side_high, side_done = (sem(n) for n in ("side_made", "side_high", "side_done"))
        xbo_done, ks_zero, ks_ready = sem("xbo_done"), sem("ks_zero"), sem("ks_ready")
        shift_done, shift2_done = sem("shift_done"), sem("shift2_done")
        w1_loaded, w2_loaded, b1_loaded, later_loaded = (
            sem(n) for n in ("w1_loaded", "w2_loaded", "b1_loaded", "later_loaded"))
        turned, high, low, b1_turned, b1_read = (sem(n) for n in ("turned", "high", "low", "b1_turned", "b1_read"))
        chain, table_ready, tails_stored, tail_ready = (
            sem(n) for n in ("chain", "table_ready", "tails_stored", "tail_ready"))
        stats2_done, moments2_done, vareps2_done, rstd2_done, xn2_done, xn2_kept = (
            sem(n) for n in ("stats2_done", "moments2_done", "vareps2_done", "rstd2_done", "xn2_done", "xn2_kept"))
        logits_made, logits_read, top_done, topi_done, gap_done, gexp_done = (
            sem(n) for n in ("logits_made", "logits_read", "top_done", "topi_done", "gap_done", "gexp_done"))
        choice_done, gsum_done, gate1_done, hot_done, load_done, counts_made, counts_read = (
            sem(n) for n in ("choice_done", "gsum_done", "gate1_done", "hot_done", "load_done", "counts_made",
                             "counts_read"))
        place_step, placeu_done = sem("place_step"), sem("placeu_done")
        goal_next, goal_set, rows_sent, step_ready = (
            sem(n) for n in ("goal_next", "goal_set", "rows_sent", "step_ready"))

        block = ctx.enter_context(nc.Block())

        def weights_bank(n):
            return s_psum[:, n % 2] if n < E else st_psum[:, n % 2]

        def store_tails(eng, first):
            eng.wait_ge(table_ready, 1)
            eng.wait_ge(tail_ready, 2)
            for e in range(first, E, 2):
                free = eng.value_load(kept.table[0:1, E + e:E + e + 1], min_val=e * REGION, max_val=e * REGION + N)
                eng.dma_start(sent[ds(free, SLOTS), :].rearrange("(h p) c -> p h c", p=P), tail[:])\
                    .then_inc(tails_stored, 16)

        x_tiles = x.rearrange("b (j p) d -> p b j d", p=P)

        @block.sync
        def _(sp):
            sp.dma_start(xres[:, 0:TILES, :], x_tiles[:, 0]).then_inc(x0_loaded, 16)
            for n, w in enumerate((Wk, Wq, Wv, Wo)):
                sp.dma_start(wraw[:, n, :], w).then_inc(w_loaded, 16)
            for n, v in enumerate((bk, bq, bv, bo)):
                sp.dma_start(rows[:, n, :], v.rearrange("(a d) -> a d", a=1)).then_inc(b_loaded, 16)
            sp.dma_start(wrraw, Wr).then_inc(b_loaded, 16)
            sp.dma_start(brrow[:], br.rearrange("(a d) -> a d", a=1)).then_inc(b_loaded, 16)
            sp.dma_start(w1raw, W1.rearrange("e (c p) d -> p (e c) d", p=P)).then_inc(w1_loaded, 16)
            sp.dma_start(w2raw, W2.rearrange("e p f -> p e f")).then_inc(w2_loaded, 16)
            sp.dma_start(b1raw, b1.rearrange("e (c p) -> (e c) p", p=P)).then_inc(b1_loaded, 16)
            for b in range(1, B):
                sp.dma_start(xres[:, TILES * b:TILES * b + TILES, :], x_tiles[:, b]).then_inc(x_loaded, 16)
            sp.dma_start(kept.beta[:], beta.rearrange("(a d) -> a d", a=1).to_broadcast([P, D])).then_inc(later_loaded, 16)

            def beat(t):
                if (q := t.every(4, -6, QUADS * B)) is not None:
                    if q < QUADS:
                        sp.wait_ge(ks_zero, q + 1)
                    t.wait(sp, side_done, SIDE["K", q] + 1, SIDES)
                    for g in range(4):
                        r = slice(32 * g, 32 * g + 32)
                        sp.dma_start(ks[r, g, q % QUADS, :].bitcast(F32), kst[r, :].bitcast(F32)).then_inc(ks_ready, 16)

            beats(sp, beat)
            sp.wait_ge(later_loaded, 16)
            store_tails(sp, 0)
            kept.count_turns("sync", sp, table_ready)
            sp.wait_ge(tails_stored, 16 * E)

        @block.gpsimd
        def _(pool):
            def first_norm(t):
                b = t.every(GROUPS, -10, B)
                t.wait(pool, moments_done, b + 1, 1)
                nc.gpsimd.tensor_tensor(vareps[:], moments[:, :, 1], eps[:], ALU.add).then_inc(vareps_done, 1)
                t.wait(pool, vareps_done, b + 1, 1)
                if b > 0:
                    t.wait(pool, xn_done, b, 1)
                nc.gpsimd.tensor_tensor(minus_mean[:], zero4[:], moments[:, :, 0], ALU.subtract)
                nc.gpsimd.tensor_tensor(rstd[:], vareps[:], power[:], ALU.pow).then_inc(rstd_done, 1)
                t.wait(pool, rstd_done, b + 1, 1)
                nc.gpsimd.tensor_tensor(shift[:], minus_mean[:], rstd[:], ALU.mult).then_inc(shift_done, 1)

            nc.gpsimd.memset(ident[:], 0.0).then_inc(ident_zero, 1)
            pool.wait_ge(ident_zero, 1)
            nc.gpsimd.affine_select(out=ident[:], in_=ident[:], compare_op=ALU.not_equal, fill=1.0, base=0,
                                    pattern=[[-1, P]], channel_multiplier=1).then_inc(ident_ready, 1)
            nc.gpsimd.memset(power[:], -0.5).then_inc(pool_consts, 1)
            nc.gpsimd.memset(zero4[:], 0.0).then_inc(pool_consts, 1)
            nc.gpsimd.memset(eps[:], EPS).then_inc(pool_consts, 1)
            pool.wait_ge(pool_consts, 3)
            first_norm(Beat(-10))
            for q in range(QUADS):
                nc.gpsimd.memset(ks[:, :, q, :].bitcast(U32), 0).then_inc(ks_zero, 1)
            nc.gpsimd.memset(mneg[:], 0.0).then_inc(pool_consts, 1)
            nc.gpsimd.memset(vst[:], 0.0).then_inc(pool_consts, 1)
            pool.wait_ge(pool_consts, 5)
            nc.gpsimd.memset(vst[:, :, :, HD:HD + 1], 1.0).then_inc(pool_consts, 1)
            nc.gpsimd.memset(tail[:], 0.0).then_inc(tail_ready, 1)
            pool.wait_ge(tail_ready, 1)
            nc.gpsimd.memset(tail[:, :, D].bitcast(U32), NOWHERE).then_inc(tail_ready, 1)
            nc.gpsimd.memset(xrow[:], 0.0)
            nc.gpsimd.memset(zero[:], 0)
            nc.gpsimd.memset(zero_e[:], 0.0)
            nc.gpsimd.memset(step[:], S)
            nc.gpsimd.iota(goal[:].bitcast(I32), [[N, 2], [P, TILES]], base=-S, channel_multiplier=1)
            nc.gpsimd.iota(iota8[:], [[1, E]], base=0, channel_multiplier=0, allow_small_or_imprecise_dtypes=True)
            nc.gpsimd.iota(origin[:], [[REGION, E]], base=0, channel_multiplier=0,
                           allow_small_or_imprecise_dtypes=True)
            nc.gpsimd.iota(fill[:], [[REGION, E]], base=0, channel_multiplier=0,
                           allow_small_or_imprecise_dtypes=True)
            nc.gpsimd.memset(ones_sq[:], 1.0).then_inc(step_ready, 1)
            pool.wait_ge(step_ready, 1)
            nc.gpsimd.affine_select(out=before[:], in_=ones_sq[:], compare_op=ALU.is_gt, fill=0.0, base=0,
                                    pattern=[[1, P]], channel_multiplier=-1).then_inc(step_ready, 1)

            def places(t, b):
                steps = [0]

                def step(out, in0, in1, op):
                    if steps[0]:
                        t.wait(pool, place_step, PLACE_STEPS * b + steps[0], PLACE_STEPS)
                    nc.gpsimd.tensor_tensor(out, in0, in1, op).then_inc(place_step, 1)
                    steps[0] += 1

                t.wait(pool, counts_read, b + 1, 1)
                step(start[:, 0, :], fill[:], zero_e[:], ALU.add)
                for j in range(TILES):
                    step(start[:, j + 1, :] if j < TILES - 1 else fill[:], start[:, j, :], counts[:, 1, j, :], ALU.add)
                step(place[:], start[:], counts[:, 0], ALU.add)
                step(picked[:], hot[:], place[:].unsqueeze(2).to_broadcast([P, TILES, 2, E]), ALU.mult)
                for half in (4, 2):
                    step(picked[:, :, :, 0:half], picked[:, :, :, 0:half], picked[:, :, :, half:2 * half], ALU.add)
                step(placef[:], picked[:, :, :, 0], picked[:, :, :, 1], ALU.add)
                assert steps[0] == PLACE_STEPS

            def beat(t):
                if t.every(GROUPS, -10, B) is not None and t.T > -10:
                    first_norm(t)

                if (b := t.every(GROUPS, -8, B)) is not None:
                    t.wait(pool, xn_done, b + 1, 1)
                    if b == 0:
                        pool.wait_ge(cols_ready, 1)
                    at = t.tiles(b)
                    nc.gpsimd.tensor_tensor(xres[:, at, :], xres[:, at, :],
                                            bob[:].unsqueeze(1).to_broadcast([P, TILES, D]), ALU.add)\
                        .then_inc(xbo_done, 1)

                if (b := t.every(GROUPS, 35, B)) is not None:
                    t.wait(pool, moments2_done, b + 1, 1)
                    nc.gpsimd.tensor_tensor(vareps2[:], moments2[:, :, 1], eps[:], ALU.add).then_inc(vareps2_done, 1)
                    t.wait(pool, vareps2_done, b + 1, 1)
                    nc.gpsimd.tensor_tensor(minus_mean2[:], zero4[:], moments2[:, :, 0], ALU.subtract)
                    nc.gpsimd.tensor_tensor(rstd2[:], vareps2[:], power[:], ALU.pow).then_inc(rstd2_done, 1)
                    t.wait(pool, rstd2_done, b + 1, 1)
                    nc.gpsimd.tensor_tensor(shift2[:], minus_mean2[:], rstd2[:], ALU.mult).then_inc(shift2_done, 1)
                if (b := t.every(GROUPS, 37, B)) is not None:
                    t.wait(pool, xn2_done, b + 1, 1)
                    nc.gpsimd.tensor_tensor(goal[:], goal[:], step[:], ALU.add).then_inc(goal_next, 1)
                    t.wait(pool, goal_next, b + 1, 1)
                    nc.gpsimd.tensor_tensor(xrow[:, :, :, D].bitcast(U32), goal[:], zero[:], ALU.add)\
                        .then_inc(goal_set, 1)
                    at = t.tiles(b)
                    if b == 0:
                        pool.wait_ge(later_loaded, 16)
                    nc.gpsimd.tensor_tensor(xres[:, at, :], xres[:, at, :], kept.beta[:].unsqueeze(1)
                                            .to_broadcast([P, TILES, D]), ALU.add)
                if (b := t.every(GROUPS, 44, B)) is not None:
                    places(t, b)
                if (b := t.every(GROUPS, 46, B)) is not None:
                    t.wait(pool, placeu_done, b + 1, 1)
                    t.wait(pool, goal_set, b + 1, 1)
                    t.wait(pool, xn2_kept, b + 1, 1)
                    nc.gpsimd.tensor_tensor(fence[:], zero[:], zero[:], ALU.add)
                    for k in range(2):
                        for j in range(TILES):
                            nc.gpsimd.indirect_dma_start(
                                out=sent, out_offset=bass.IndirectOffsetOnAxis(ap=placeu[:, j, k:k + 1], axis=0),
                                in_=xrow[:, k, j, :], in_offset=None).then_inc(rows_sent, 16)

            for T in range(FIRST_BEAT, LOOP_FROM):
                beat(Beat(T))
            with pool.Fori(0, LOOPS) as turn:
                for T in range(LOOP_FROM, LOOP_FROM + GROUPS):
                    beat(Beat(T, turn))
            for T in range(LOOP_FROM + GROUPS * LOOPS, LAST_BEAT + 1):
                beat(Beat(T))
            kept.count_turns("gpsimd", pool, table_ready)
            pool.wait_ge(rows_sent, 16 * 2 * TILES * B)

        @block.scalar
        def _(act):
            act.wait_ge(consts_ready, 1)
            act.wait_ge(w_turned, 1)
            for n in range(2):
                for r in range(3):
                    nc.scalar.copy(
                        wh[:, n].rearrange("p c (g r d) -> p c g r d", g=4, d=HD)[:, :, :, r, :],
                        side_psum[:, 0, P * n:P * n + P].rearrange("p (c g d) -> p c g d", c=QUADS, d=HD))
            nc.scalar.copy(wvh[:], side_psum[:, 0, 2 * P:3 * P])
            nc.scalar.copy(woh[:], side_psum[:, 0, 3 * P:4 * P]).then_inc(w_high, 1)

            def beat(t):
                if (q := t.every(4, 11, QUADS * B)) is not None:
                    t.wait(act, pv_made, 4 * q + 4, GROUPS)
                    if q >= 2:
                        t.wait(act, o_turned, q - 1, QUADS)
                    nc.scalar.copy(pvs[:, q % 2, :], pv_psum[:, 0, :]).then_inc(pv_copied, 1)
                n = t.st()
                for g in range(4):
                    if n is not None:
                        k = 4 * n + g
                        t.wait(act, st_made, k + 1, 4 * GROUPS)
                        if n >= PT_SLOTS and g == 0:
                            t.wait(act, pv_made, n - PT_SLOTS + 1, GROUPS)
                        nc.scalar.activation(pt[:, n % PT_SLOTS, g, :], st_psum[:, k % ST_BANKS, :], ACT.Exp,
                                             scale=SCALE).then_inc(exp_done, 1)
                    if g == 1 and side_task(t.T):
                        kind, of = side_task(t.T)
                        i = SIDE[kind, of]
                        if kind in ("K", "Q"):
                            w = 0 if kind == "K" else 1
                            c = of % QUADS
                            col = 2 * QUADS + w
                            t.wait(act, side_made, i + 1, SIDES)
                            nc.scalar.activation(hm[:], side_psum[:, 0, :], ACT.Identity,
                                                 bias=bmask[:, QUADS * w + c:QUADS * w + c + 1],
                                                 scale=bcol[:, col:col + 1]).then_inc(side_high, 1)
                        elif kind == "X2T":
                            t.wait(act, side_made, i + 1, SIDES)
                            nc.scalar.copy(xt2[:], side_psum[:, 0, :]).then_inc(side_done, 1)
                        elif kind == "XT":
                            t.wait(act, side_made, i + 1, SIDES)
                            nc.scalar.copy(xth[:], side_psum[:, 0, :]).then_inc(side_high, 1)
                        elif kind == "OT":
                            t.wait(act, side_made, i + 1, SIDES)
                            nc.scalar.copy(oth[:], side_psum[:, 0, :]).then_inc(side_high, 1)

            def beat_and_gates(t):
                if t.T == -8:
                    act.wait_ge(cols_ready, 1)
                beat(t)
                if (b := t.every(GROUPS, 41, B)) is not None:
                    t.wait(act, gap_done, b + 1, 1)
                    nc.scalar.activation(gexp[:], gap[:], ACT.Exp).then_inc(gexp_done, 1)

                if (b := t.every(GROUPS, -9, B)) is not None:
                    t.wait(act, shift_done, b + 1, 1)
                    for j in range(TILES):
                        ins = nc.scalar.activation(xn[:, j:j + 1, :], xres[:, t.tiles(b, j, 1), :], ACT.Identity,
                                                   bias=shift[:, j:j + 1], scale=rstd[:, j:j + 1])
                    ins.then_inc(xn_done, 1)
                if (b := t.every(GROUPS, 36, B)) is not None:
                    if b > 0:
                        t.wait(act, rows_sent, 16 * 2 * TILES * b, 16 * 2 * TILES)
                    else:
                        act.wait_ge(step_ready, 2)
                    t.wait(act, shift2_done, b + 1, 1)
                    for j in range(TILES):
                        ins = nc.scalar.activation(xrow[:, 0, j:j + 1, 0:D], xres[:, t.tiles(b, j, 1), :],
                                                   ACT.Identity, bias=shift2[:, j:j + 1], scale=rstd2[:, j:j + 1])
                    ins.then_inc(xn2_done, 1)
                if (b := t.every(GROUPS, 37, B)) is not None:
                    t.wait(act, xn2_done, b + 1, 1)
                    nc.scalar.copy(xrow[:, 1, :, 0:D], xrow[:, 0, :, 0:D])
                    nc.scalar.copy(kept.xn2[:, t.tiles(b), :], xrow[:, 0, :, 0:D]).then_inc(xn2_kept, 1)
                for n in expert_weights(t):
                    act.wait_ge(turned, n + 1)
                    src = weights_bank(n).rearrange("p (c d) -> p c d", c=FC)
                    dst = kept.w1h if n < E else kept.w2t
                    at = FC * (n % E)
                    nc.scalar.copy(dst[:, at:at + FC, :], src).then_inc(high, 1)

            beats(act, beat_and_gates)
            store_tails(act, 1)
            kept.count_turns("scalar", act, table_ready)

        high_before = {}
        for task, i in sorted(SIDE.items(), key=lambda kv: kv[1]):
            high_before[task] = sum(1 for (kind, _), j in SIDE.items() if j <= i and kind in ("K", "Q", "XT", "OT"))

        @block.vector
        def _(dve):
            nc.vector.memset(wh[:].bitcast(U32), 0)
            nc.vector.memset(wl[:].bitcast(U32), 0)
            nc.vector.memset(brow, 0.0)
            nc.vector.memset(mrow, 0.0)
            nc.vector.memset(ones[:], 1.0).then_inc(consts_ready, 1)

            def statistics(t, b):
                for j in range(TILES):
                    ins = nc.vector.bn_stats(stats[:, j, :], xres[:, t.tiles(b, j, 1), :])
                ins.then_inc(stats_done, 1)

            def mean_and_variance():
                for j in range(TILES):
                    ins = nc.vector.bn_aggr(moments[:, j, :], stats[:, j, :])
                ins.then_inc(moments_done, 1)

            dve.wait_ge(x0_loaded, 16)
            statistics(Beat(-11), 0)
            dve.wait_ge(stats_done, 1)
            mean_and_variance()
            dve.wait_ge(consts_ready, 1)
            dve.wait_ge(b_loaded, 96)
            for n in range(2):
                for r in range(3):
                    nc.vector.tensor_copy(
                        brow[:, n].rearrange("p c (g r d) -> p c g r d", g=4, d=HD)[:, :, :, r, :],
                        rows[:, n, :].rearrange("p (c g d) -> p c g d", c=QUADS, d=HD))
            nc.vector.memset(brow[:, 0].rearrange("p c (g r) -> p c g r", g=4)[:, :, :, SHIFT_ROW], 1.0)
            for n, r in ((0, 2), (1, 1)):
                nc.vector.memset(mrow[:, n].rearrange("p (g r) -> p g r", g=4)[:, :, HD * r:HD * r + HD], 1.0)\
                    .then_inc(rows_ready, 1)
            dve.wait_ge(w_high, 1)
            for n in range(2):
                for r in range(3):
                    def stack(w):
                        return w[:, n].rearrange("p c (g r d) -> p c g r d", g=4, d=HD)[:, :, :, r, :]
                    nc.vector.tensor_tensor(
                        stack(wl), side_psum[:, 0, P * n:P * n + P].rearrange("p (c g d) -> p c g d", c=QUADS, d=HD),
                        stack(wh).bitcast(F32), ALU.subtract)
            nc.vector.tensor_tensor(wvl[:], side_psum[:, 0, 2 * P:3 * P], wvh[:].bitcast(F32), ALU.subtract)
            nc.vector.tensor_tensor(wol[:], side_psum[:, 0, 3 * P:4 * P], woh[:].bitcast(F32), ALU.subtract)\
                .then_inc(w_ready, 1)
            dve.wait_ge(cols_made, 1)
            nc.vector.tensor_copy(bcol[:], turn_psum[:, 0, 0:2 * QUADS + 2]).then_inc(setup_used, 1)
            nc.vector.tensor_copy(bvb[:], turn_psum[:, 0, 128:256])
            nc.vector.tensor_copy(bob[:], turn_psum[:, 0, 256:384])
            nc.vector.tensor_copy(brb[:], turn_psum[:, 0, 384:384 + E])
            nc.vector.tensor_copy(wrt[:], turn_psum[:, 0, 400:400 + E])
            dve.wait_ge(setup_used, 1)
            for n in range(2):
                ins = nc.vector.tensor_scalar(bmask[:, QUADS * n:QUADS * n + QUADS],
                                              bcol[:, QUADS * n:QUADS * n + QUADS],
                                              bcol[:, 2 * QUADS + n:2 * QUADS + n + 1], None, ALU.mult)
            ins.then_inc(cols_ready, 1)

            def maxima(t, g):
                n = t.scores()
                if n is None:
                    return
                k = 4 * n + g
                t.wait(dve, s_made, k + 1, 4 * GROUPS)
                if n == 0 and g == 0:
                    dve.wait_ge(pool_consts, 6)
                nc.vector.tensor_reduce(mneg[:, (n // 4) % 2, n % 4, 32 * g + SHIFT_ROW:32 * g + SHIFT_ROW + 1],
                                        s_psum[:, s_bank(k), :], AX_X, ALU.max, negate=True).then_inc(max_done, 1)

            def beat(t):
                if (b := t.every(GROUPS, -10, B)) is not None and b > 0:
                    t.wait(dve, stats_done, b + 1, 1)
                if (b := t.every(GROUPS, 34, B)) is not None:
                    t.wait(dve, side_done, SIDE["O", b] + 1, SIDES)
                if (b := t.every(GROUPS, 35, B)) is not None:
                    t.wait(dve, stats2_done, b + 1, 1)
                if (b := t.every(GROUPS, 40, B)) is not None:
                    t.wait(dve, logits_read, b + 1, 1)
                if (b := t.every(GROUPS, 41, B)) is not None:
                    t.wait(dve, top_done, b + 1, 1)
                maxima(t, 0)
                maxima(t, 1)
                if (q := t.every(4, 4, QUADS * B)) is not None:
                    c = q % QUADS
                    t.wait(dve, shift_turned, q + 1, QUADS)
                    nc.vector.tensor_tensor(qs[:, c, :], turn_psum[:, 0, :], qs[:, c, :].bitcast(F32), ALU.add)\
                        .then_inc(shift_added, 1)
                if (q := t.every(4, 14, QUADS * B)) is not None:
                    c = q % QUADS
                    t.wait(dve, o_turned, q + 1, QUADS)
                    sums = turn_psum[:, 0, :].rearrange("p (j g r) -> p j g r", j=TILES, g=4)
                    nc.vector.reciprocal(rden[:], sums[:, :, :, HD]).then_inc(rden_done, 1)
                    t.wait(dve, rden_done, q + 1, QUADS)
                    nc.vector.tensor_tensor(
                        onorm[:].rearrange("p j (h d) -> p j h d", d=HD)[:, :, 4 * c:4 * c + 4, :],
                        sums[:, :, :, 0:HD], rden[:].unsqueeze(3).to_broadcast([P, TILES, 4, HD]),
                        ALU.mult).then_inc(o_normed, 1)
                maxima(t, 2)
                maxima(t, 3)
                if side_task(t.T):
                    kind, of = side_task(t.T)
                    i = SIDE[kind, of]
                    if kind in ("K", "Q"):
                        c = of % QUADS
                        w = 0 if kind == "K" else 1
                        if of >= QUADS:
                            t.wait(dve, st_made, 16 * (of - QUADS) + 16, 4 * GROUPS)
                        if kind == "K" and of > 0:
                            t.wait(dve, ks_ready, 64 * of, 64 * QUADS)
                        t.wait(dve, side_high, high_before[kind, of], HIGHS)
                        nc.vector.scalar_tensor_tensor(
                            out=kst[:] if kind == "K" else qs[:, c, :], in0=side_psum[:, 0, :],
                            scalar=bcol[:, QUADS * w + c:QUADS * w + c + 1], in1=hm[:].bitcast(F32),
                            op0=ALU.add, op1=ALU.subtract).then_inc(side_done, 1)
                    elif kind in ("XT", "OT"):
                        hi, lo = (xth, xtl) if kind == "XT" else (oth, otl)
                        t.wait(dve, side_high, high_before[kind, of], HIGHS)
                        nc.vector.tensor_tensor(lo[:], side_psum[:, 0, :], hi[:].bitcast(F32), ALU.subtract)\
                            .then_inc(side_done, 1)
                    elif kind == "V":
                        c = of % 2
                        t.wait(dve, side_made, i + 1, SIDES)
                        if of < 2:
                            dve.wait_ge(pool_consts, 6)
                        nc.vector.tensor_tensor(
                            vst[:, :, 8 * c:8 * c + 8, 0:HD],
                            side_psum[:, 0, 0:2 * P].rearrange("p (j g d) -> p j g d", j=TILES, d=HD),
                            bvb[:, 64 * c:64 * c + 64].rearrange("p (g d) -> p g d", d=HD).unsqueeze(1)
                            .to_broadcast([P, TILES, 8, HD]), ALU.add).then_inc(side_done, 1)
                    elif kind == "O":
                        t.wait(dve, side_made, i + 1, SIDES)
                        t.wait(dve, xbo_done, of + 1, 1)
                        at = t.tiles(of)
                        nc.vector.tensor_tensor(
                            xres[:, at, :], side_psum[:, 0, :].rearrange("p (j d) -> p j d", j=TILES),
                            xres[:, at, :], ALU.add).then_inc(side_done, 1)
                if (b := t.every(GROUPS, -11, B)) is not None and b > 0:
                    dve.wait_ge(x_loaded, 16 * (B - 1))
                    statistics(t, b)
                if (b := t.every(GROUPS, -10, B)) is not None and b > 0:
                    mean_and_variance()
                route(t)
                for n in expert_weights(t):
                    if n < E:
                        dve.wait_ge(high, n + 1)
                        at = slice(FC * n, FC * n + FC)
                        nc.vector.tensor_tensor(kept.w1l[:, at, :], weights_bank(n).rearrange("p (c d) -> p c d", c=FC),
                                                kept.w1h[:, at, :].bitcast(F32), ALU.subtract).then_inc(low, 1)
                if t.T == 2:
                    dve.wait_ge(b1_turned, 1)
                    nc.vector.tensor_copy(kept.b1c[:], turn_psum[:, 0, 0:E * FC]).then_inc(b1_read, 1)

            def route(t):
                if (b := t.every(GROUPS, 34, B)) is not None:
                    for j in range(TILES):
                        ins = nc.vector.bn_stats(stats2[:, j, :], xres[:, t.tiles(b, j, 1), :])
                    ins.then_inc(stats2_done, 1)
                if t.every(GROUPS, 35, B) is not None:
                    for j in range(TILES):
                        ins = nc.vector.bn_aggr(moments2[:, j, :], stats2[:, j, :])
                    ins.then_inc(moments2_done, 1)
                if (b := t.every(GROUPS, 39, B)) is not None:
                    t.wait(dve, logits_made, b + 1, 1)
                    nc.vector.tensor_tensor(
                        logits[:], turn_psum[:, 0, 0:TILES * E].rearrange("p (j e) -> p j e", e=E),
                        brb[:].unsqueeze(1).to_broadcast([P, TILES, E]), ALU.add).then_inc(logits_read, 1)
                if t.every(GROUPS, 40, B) is not None:
                    for j in range(TILES):
                        ins = nc.vector.max(top[:, j, :], logits[:, j, :])
                    ins.then_inc(top_done, 1)
                if t.every(GROUPS, 41, B) is not None:
                    nc.vector.tensor_tensor(gap[:], top[:, :, 1], top[:, :, 0], ALU.subtract).then_inc(gap_done, 1)
                    for j in range(TILES):
                        ins = nc.vector.max_index(topi[:, j, :], top[:, j, :], logits[:, j, :])
                    ins.then_inc(topi_done, 1)
                if (b := t.every(GROUPS, 42, B)) is not None:
                    t.wait(dve, gexp_done, b + 1, 1)
                    nc.vector.tensor_scalar_add(gsum[:], gexp[:], 1.0).then_inc(gsum_done, 1)
                    t.wait(dve, topi_done, b + 1, 1)
                    nc.vector.tensor_copy(choice[:], topi[:, :, 0:2]).then_inc(choice_done, 1)
                    t.wait(dve, choice_done, b + 1, 1)
                    nc.vector.tensor_tensor(hot[:], iota8[:].unsqueeze(1).unsqueeze(1).to_broadcast([P, TILES, 2, E]),
                                            choice[:].unsqueeze(3).to_broadcast([P, TILES, 2, E]), ALU.is_equal)\
                        .then_inc(hot_done, 1)
                    t.wait(dve, gsum_done, b + 1, 1)
                    nc.vector.reciprocal(gsum[:], gsum[:]).then_inc(gate1_done, 1)
                    t.wait(dve, hot_done, b + 1, 1)
                    nc.vector.tensor_tensor(load[:], hot[:, :, 0, :], hot[:, :, 1, :], ALU.add).then_inc(load_done, 1)
                    t.wait(dve, gate1_done, b + 1, 1)
                    nc.vector.tensor_copy(xrow[:, 0, :, D + 1], gsum[:])
                    nc.vector.tensor_tensor(xrow[:, 1, :, D + 1], gsum[:], gexp[:], ALU.mult)
                if (b := t.every(GROUPS, 43, B)) is not None:
                    t.wait(dve, counts_made, b + 1, 1)
                    nc.vector.tensor_copy(counts[:], turn_psum[:, 0, 0:2 * TILES * E].rearrange(
                        "p (a j e) -> p a j e", a=2, e=E)).then_inc(counts_read, 1)
                if (b := t.every(GROUPS, 45, B)) is not None:
                    t.wait(dve, place_step, PLACE_STEPS * (b + 1), PLACE_STEPS)
                    nc.vector.tensor_copy(placeu[:], placef[:]).then_inc(placeu_done, 1)

            beats(dve, beat)

            steps = [0]

            def link(ins):
                steps[0] += 1
                ins.then_inc(chain, 1)
                dve.wait_ge(chain, steps[0])

            link(nc.vector.tensor_tensor(tokens[:], fill[:], origin[:], ALU.subtract))
            link(nc.vector.tensor_scalar_add(tokens[:], tokens[:], float(SLOTS - 1)))
            link(nc.vector.tensor_copy(tokens_i[:], tokens[:]))
            link(nc.vector.tensor_scalar(tokens_i[:], tokens_i[:], SLOTS.bit_length() - 1, None, ALU.arith_shift_right))
            link(nc.vector.tensor_copy(tokens[:], tokens_i[:]))
            link(nc.vector.tensor_scalar(tokens[:], tokens[:], 1.0, None, ALU.max))
            nc.vector.tensor_copy(kept.table[:, 0:E], tokens[:])
            nc.vector.tensor_copy(kept.table[:, E:2 * E], fill[:]).then_inc(table_ready, 1)
            kept.count_turns("vector", dve, table_ready)

        @block.tensor
        def _(pe):
            mm = nc.tensor.matmul

            def split3(dst, ah, al, bh, bl):
                mm(dst, ah, bh, start=True, stop=False)
                mm(dst, al, bh, start=False, stop=False)
                return mm(dst, ah, bl, start=False, stop=True)

            pe.wait_ge(ident_ready, 1)
            pe.wait_ge(w_loaded, 64)
            for n in range(4):
                ins = nc.tensor.transpose(side_psum[:, 0, P * n:P * n + P], wraw[:, n, :], ident[:])
            ins.then_inc(w_turned, 1)
            pe.wait_ge(rows_ready, 2)
            for n in range(2):
                for c in range(QUADS):
                    mm(turn_psum[:, 0, QUADS * n + c:QUADS * n + c + 1], brow[:, n, c, :], ones[:, 0:1],
                       start=True, stop=True)
            for n in range(2):
                mm(turn_psum[:, 0, 2 * QUADS + n:2 * QUADS + n + 1], mrow[:, n, :], ones[:, 0:1], start=True, stop=True)
            mm(turn_psum[:, 0, 384:384 + E], ones[:], brrow[:], start=True, stop=True)
            nc.tensor.transpose(turn_psum[:, 0, 400:400 + E], wrraw, ident[0:E, 0:E])
            for n in (2, 3):
                ins = mm(turn_psum[:, 0, 128 * (n - 1):128 * n], ones[:], rows[:, n, :], start=True, stop=True)
            ins.then_inc(cols_made, 1)
            pe.wait_ge(w_ready, 1)
            pe.wait_ge(cols_ready, 1)

            def scores(t, g):
                n = t.scores()
                if n is None:
                    return
                k, q = 4 * n + g, n // 4
                if n % 4 == 0 and g == 0:
                    t.wait(pe, ks_ready, 64 * (q + 1), 64 * QUADS)
                    t.wait(pe, side_done, SIDE["Q", q] + 1, SIDES)
                if k == 0:
                    pe.wait_ge(high, E)
                    pe.wait_ge(low, E)
                if s_bank_last_user(k) >= 0:
                    t.wait(pe, max_done, s_bank_last_user(k) + 1, 4 * GROUPS)
                mm(s_psum[:, s_bank(k), :], qs[:, q % QUADS, P * (n % 4):P * (n % 4) + P], ks[:, g, q % QUADS, :],
                   start=True, stop=True).then_inc(s_made, 1)

            def scores_t(t, g):
                n = t.st()
                if n is None:
                    return
                k, q = 4 * n + g, n // 4
                if n % 4 == 0 and g == 0:
                    t.wait(pe, shift_added, q + 1, QUADS)
                if k == 0:
                    pe.wait_ge(high, 2 * E)
                if k >= ST_BANKS:
                    t.wait(pe, exp_done, k - ST_BANKS + 1, 4 * GROUPS)
                mm(st_psum[:, k % ST_BANKS, :], ks[:, g, q % QUADS, P * (n % 4):P * (n % 4) + P], qs[:, q % QUADS, :],
                   start=True, stop=True).then_inc(st_made, 1)

            def turn(t):
                if (q := t.every(4, 4, QUADS * B)) is not None:
                    t.wait(pe, max_done, 16 * q + 16, 4 * GROUPS)
                    if q - 2 > 0:
                        t.wait(pe, o_normed, q - 2, QUADS)
                    if (b := t.every(GROUPS, 40, B)) is not None:
                        t.wait(pe, logits_read, b + 1, 1)
                    if (b := t.every(GROUPS, 44, B)) is not None:
                        t.wait(pe, counts_read, b + 1, 1)
                    if q == 0:
                        pe.wait_ge(b1_read, 1)
                    for j in range(TILES):
                        ins = nc.tensor.transpose(turn_psum[:, 0, P * j:P * j + P], mneg[:, q % 2, j, :], ident[:])
                    ins.then_inc(shift_turned, 1)
                if (q := t.every(4, 14, QUADS * B)) is not None:
                    t.wait(pe, pv_copied, q + 1, QUADS)
                    if isinstance(t.turn, int) and (b := t.every(GROUPS, 42, B)) is not None:
                        t.wait(pe, logits_read, b + 1, 1)
                    if q + 3 <= QUADS * B:
                        t.wait(pe, shift_added, q + 3, QUADS)
                    else:
                        t.wait(pe, o_normed, q, QUADS)
                    for j in range(TILES):
                        ins = nc.tensor.transpose(turn_psum[:, 0, P * j:P * j + P], pvs[:, q % 2, P * j:P * j + P],
                                                  ident[:])
                    ins.then_inc(o_turned, 1)
                if (b := t.every(GROUPS, 39, B)) is not None:
                    t.wait(pe, side_done, SIDE["X2T", b] + 1, SIDES)
                    t.wait(pe, o_normed, min(QUADS * b + 7, QUADS * B), QUADS)
                    if isinstance(t.turn, int) and b > 0:
                        t.wait(pe, counts_read, b, 1)
                    for j in range(TILES):
                        ins = mm(turn_psum[:, 0, E * j:E * j + E], xt2[:, P * j:P * j + P], wrt[:],
                                 start=True, stop=True)
                    ins.then_inc(logits_made, 1)
                if (b := t.every(GROUPS, 43, B)) is not None:
                    t.wait(pe, load_done, b + 1, 1)
                    t.wait(pe, o_normed, min(QUADS * b + 8, QUADS * B), QUADS)
                    flat = load[:].rearrange("p j e -> p (j e)")
                    mm(turn_psum[:, 0, 0:TILES * E], before[:], flat, start=True, stop=True)
                    mm(turn_psum[:, 0, TILES * E:2 * TILES * E], ones_sq[:], flat, start=True, stop=True)\
                        .then_inc(counts_made, 1)

            def side(t):
                if not side_task(t.T):
                    return
                kind, of = side_task(t.T)
                i = SIDE[kind, of]
                t.wait(pe, side_done, i, SIDES)
                c = of % QUADS
                if kind == "XT":
                    t.wait(pe, xn_done, of + 1, 1)
                    for j in range(TILES):
                        ins = nc.tensor.transpose(side_psum[:, 0, P * j:P * j + P], xn[:, j, :], ident[:])
                elif kind in ("K", "Q"):
                    w = 0 if kind == "K" else 1
                    ins = split3(side_psum[:, 0, :], wh[:, w, c, :], wl[:, w, c, :], xth[:], xtl[:])
                elif kind == "X2T":
                    t.wait(pe, xn2_done, of + 1, 1)
                    for j in range(TILES):
                        ins = nc.tensor.transpose(side_psum[:, 0, P * j:P * j + P], xrow[:, 0, j, 0:D], ident[:])
                elif kind == "V":
                    for j in range(TILES):
                        cols = slice(64 * (of % 2), 64 * (of % 2) + 64)
                        ins = split3(side_psum[:, 0, 64 * j:64 * j + 64], xth[:, P * j:P * j + P],
                                     xtl[:, P * j:P * j + P], wvh[:, cols], wvl[:, cols])
                elif kind == "OT":
                    t.wait(pe, o_normed, QUADS * (of + 1), QUADS)
                    for j in range(TILES):
                        ins = nc.tensor.transpose(side_psum[:, 0, P * j:P * j + P], onorm[:, j, :], ident[:])
                else:
                    for j in range(TILES):
                        ins = split3(side_psum[:, 0, P * j:P * j + P], oth[:, P * j:P * j + P],
                                     otl[:, P * j:P * j + P], woh[:], wol[:])
                ins.then_inc(side_made, 1)

            def values(t):
                n = t.pv()
                if n is None:
                    return
                q = n // 4
                t.wait(pe, exp_done, 4 * n + 4, 4 * GROUPS)
                if n % 4 == 0:
                    t.wait(pe, side_done, SIDE["V", q // 2] + 1, SIDES)
                    if q > 0:
                        t.wait(pe, pv_copied, q, QUADS)
                for g in range(4):
                    ins = mm(pv_psum[32 * g:32 * g + 32, 0, :], vst[:, n % 4, 4 * (q % QUADS) + g, :],
                             pt[:, n % PT_SLOTS, g, :], start=(n % 4 == 0), stop=(n % 4 == 3))
                ins.then_inc(pv_made, 1)

            def beat(t):
                scores(t, 0)
                scores_t(t, 0)
                scores(t, 1)
                scores_t(t, 1)
                scores(t, 2)
                turn(t)
                side(t)
                scores_t(t, 2)
                scores(t, 3)
                scores_t(t, 3)
                values(t)
                for n in expert_weights(t):
                    if n % E == 0:
                        pe.wait_ge((w1_loaded, w2_loaded)[n // E], 16)
                    if n >= 2:
                        pe.wait_ge(high, n - 1)
                        pe.wait_ge(low, min(n - 1, E))
                    for c in range(FC):
                        src = w1raw[:, FC * n + c, :] if n < E else w2raw[:, n - E, P * c:P * c + P]
                        ins = nc.tensor.transpose(weights_bank(n)[:, P * c:P * c + P], src, ident[:])
                    ins.then_inc(turned, 1)
                if t.T == 2:
                    pe.wait_ge(b1_loaded, 16)
                    nc.tensor.transpose(turn_psum[:, 0, 0:E * FC], b1raw, ident[0:E * FC, 0:E * FC])\
                        .then_inc(b1_turned, 1)

            beats(pe, beat)
            kept.count_turns("tensor", pe, table_ready)


def experts(nc, gamma, b2, kept, sent, results, unread, out):
    with ExitStack() as ctx:
        def sb(name, shape, dt=F32):
            return ctx.enter_context(nc.sbuf_tensor(name, shape, dt))

        def sem(name):
            return ctx.enter_context(nc.semaphore(name))

        def psum(name, banks=1):
            return ctx.enter_context(nc.psum_tensor(name, [P, banks, 512], F32))

        ident, w1h, w1l, w2t, b1c = kept.ident, kept.w1h, kept.w1l, kept.w2t, kept.b1c
        gammab, b2b = sb("gammab", [P, D]), sb("b2b", [P, E, D])
        eps2, power2 = sb("eps2", [P, TILES]), sb("power2", [P, TILES])
        lot = sb("lot", [P, HALVES, ROW])
        goals = sb("goals", [P, GOALS, HALVES, 2], U32)
        ysum = sb("ysum", [P, HALVES, D])
        xh, xl = sb("xh", [P, SLOTS], F32R), sb("xl", [P, SLOTS], F32R)
        hid = sb("hid", [P, FC, SLOTS])
        res = sb("res", [P, HALVES, D])
        goal_now = sb("goal_now", [P, HALVES], U32)
        zero2 = sb("zero2", [P, HALVES], U32)
        fence2 = sb("fence2", [P, HALVES], U32)
        got = sb("got", [P, 2, TILES * B, D])
        z1 = sb("z1", [P, TILES, D])
        z = sb("z", [P, 2, TILES, D])
        stats3 = sb("stats3", [P, 2, TILES, 6])
        moments3 = sb("moments3", [P, 2, TILES, 2])
        vareps3, rstd3 = sb("vareps3", [P, 2, TILES]), sb("rstd3", [P, 2, TILES])
        zero4, minus_mean, shift3 = sb("zero4b", [P, TILES]), sb("minus_mean3", [P, 2, TILES]), sb("shift3", [P, 2, TILES])
        normed = sb("normed", [P, 2, TILES, D])
        scaled = sb("scaled", [P, 2, TILES, D])

        h_psum = psum("h_psum", FC)
        y_psum = psum("y_psum", HALVES)
        x_psum = psum("x_psum")

        const_ready, b2_loaded, y_summed = sem("const_ready"), sem("b2_loaded"), sem("y_summed")
        rows_stored = [sem(f"rows_stored{h}") for h in range(HALVES)]
        lot_loaded, lot_turned, goals_taken, goals_now = (
            sem(n) for n in ("lot_loaded", "lot_turned", "goals_taken", "goals_now"))
        xh_done, xl_done, h_made, relu_act, relu_dve, y_made, y_done = (
            sem(n) for n in ("xh_done", "xl_done", "h_made", "relu_act", "relu_dve", "y_made", "y_done"))
        got_in = [sem("got_in_even"), sem("got_in_odd")]
        z1_done, z_done, s3_done, m3_done, v3_done, r3_done = (
            sem(n) for n in ("z1_done", "z_done", "s3_done", "m3_done", "v3_done", "r3_done"))
        n_done, g_done, fin_done, stored, shift_done = (
            sem(n) for n in ("n_done", "g_done", "fin_done", "stored", "shift3_done"))

        block = ctx.enter_context(nc.Block())

        def counts_of(name, eng):
            turns = kept.turns[name]
            first = [0]
            for e in range(E):
                first.append(eng.snap(turns[e] + first[e], min_val=e + 1, max_val=LOTS))
            return turns, first

        LOTS = 2 * N // SLOTS + E
        sent_e = sent.rearrange("(e r) c -> e r c", e=E)

        def stored_count(lots):
            return lots * 16 + 16

        @block.sync
        def _(sp):
            turns, first = counts_of("sync", sp)

            def load(v, src):
                sp.wait_ge(lot_turned, v + 1)
                sp.wait_ge(goals_taken, v + 1)
                sp.dma_start(lot[:], src.rearrange("(h p) c -> p h c", p=P)).then_inc(lot_loaded, 16)

            for e in range(E):
                with sp.Fori(0, turns[e]) as i:
                    at = sp.snap(i * SLOTS, min_val=0, max_val=N - SLOTS)
                    v = sp.snap(first[e] + i, min_val=0, max_val=LOTS)
                    load(v, sent_e[e, ds(at, SLOTS), :])
            total = first[E]
            load(total, sent_e[0, 0:SLOTS, :])
            got_from = results.rearrange("(k t p) d -> p k t d", k=2, p=P)

            def fetch(at, parity):
                for k in range(2):
                    sp.dma_start(got[:, k, at, :], got_from[:, k, at, :]).then_inc(got_in[parity], 16)

            for h in range(HALVES):
                sp.wait_ge(rows_stored[h], stored_count(total))
            for b in range(2):
                fetch(slice(b * TILES, b * TILES + TILES), b)
            with sp.Fori(1, B // 2) as pair:
                for parity in range(2):
                    at = sp.snap((pair * 2 + parity) * TILES, min_val=2 * TILES, max_val=(B - 1) * TILES)
                    sp.wait_ge(got_in[parity], pair * 32)
                    fetch(ds(at, TILES), parity)
            out_tiles = out.rearrange("b (j p) d -> p b j d", p=P)
            with sp.Fori(0, B) as b:
                to = sp.snap(b + 0, min_val=0, max_val=B - 1)
                at = sp.snap(b * TILES, min_val=0, max_val=(B - 1) * TILES)
                sp.wait_ge(fin_done, b + 1)
                sp.dma_start(out_tiles[:, ds(to, 1)], got[:, 0:1, ds(at, TILES), :]).then_inc(stored, 16)
            sp.wait_ge(stored, 16 * B)

        @block.gpsimd
        def _(pool):
            nc.gpsimd.memset(eps2[:], EPS)
            nc.gpsimd.memset(power2[:], -0.5)
            nc.gpsimd.memset(zero2[:], 0).then_inc(const_ready, 1)
            nc.gpsimd.memset(zero4[:], 0.0).then_inc(const_ready, 1)
            pool.wait_ge(const_ready, 2)
            for h in range(HALVES):
                pool.dma_start(unread[h:h + 1, :], zero4[0:1, :]).then_inc(rows_stored[h], stored_count(0))
            turns, first = counts_of("gpsimd", pool)
            for e in range(E):
                with pool.Fori(0, turns[e]) as i:
                    u = first[e] + i
                    for h in range(HALVES):
                        pool.wait_ge(rows_stored[h], stored_count(u))
                        pool.wait_ge(goals_taken, u + 2)
                        nc.gpsimd.tensor_tensor(goal_now[:, h:h + 1], goals[:, u & (GOALS - 1), h, 0:1],
                                                zero2[:, 0:1], ALU.add).then_inc(goals_now, 1)
                        pool.wait_ge(goals_now, u * HALVES + h + 1)
                        pool.wait_ge(y_done, u * HALVES + h + 1)
                        nc.gpsimd.tensor_tensor(fence2[:], zero2[:], zero2[:], ALU.add)
                        nc.gpsimd.indirect_dma_start(
                            out=results, out_offset=bass.IndirectOffsetOnAxis(
                                ap=goal_now[:, h:h + 1], axis=0),
                            in_=res[:, h, :], in_offset=None, bounds_check=2 * N - 1, oob_is_err=False)\
                            .then_inc(rows_stored[h], 16)

            def scale(b, parity):
                pool.wait_ge(m3_done, b + 1)
                nc.gpsimd.tensor_tensor(vareps3[:, parity], moments3[:, parity, :, 1], eps2[:], ALU.add).then_inc(v3_done, 1)
                nc.gpsimd.tensor_tensor(minus_mean[:, parity], zero4[:], moments3[:, parity, :, 0], ALU.subtract)\
                    .then_inc(v3_done, 1)
                pool.wait_ge(v3_done, b * 2 + 2)
                nc.gpsimd.tensor_tensor(rstd3[:, parity], vareps3[:, parity], power2[:], ALU.pow).then_inc(r3_done, 1)
                pool.wait_ge(r3_done, b + 1)
                nc.gpsimd.tensor_tensor(shift3[:, parity], minus_mean[:, parity], rstd3[:, parity], ALU.mult)\
                    .then_inc(shift_done, 1)

            def total_of(b, parity):
                pool.wait_ge(g_done, b + 1)
                at = tiles(b)
                nc.gpsimd.tensor_tensor(got[:, 0, at, :], scaled[:, parity], kept.xres[:, at, :], ALU.add)\
                    .then_inc(fin_done, 1)

            scale(0, 0)
            scale(1, 1)
            with pool.Fori(1, B // 2) as pair:
                for parity in range(2):
                    scale(pair * 2 + parity, parity)
                    total_of(pair * 2 + parity - 2, parity)
            total_of(B - 2, 0)
            total_of(B - 1, 1)

        @block.scalar
        def _(act):
            act.wait_ge(lot_loaded, 16)
            act.dma_start(b2b[:], b2.rearrange("(a e) d -> a e d", a=1).to_broadcast([P, E, D])).then_inc(b2_loaded, 16)
            act.dma_start(gammab[:], gamma.rearrange("(a d) -> a d", a=1).to_broadcast([P, D])).then_inc(b2_loaded, 16)
            turns, first = counts_of("scalar", act)

            def split_high(count):
                act.wait_ge(lot_turned, count)
                nc.scalar.copy(xh[:], x_psum[:, 0, 0:SLOTS]).then_inc(xh_done, 1)

            split_high(2)
            for e in range(E):
                with act.Fori(0, turns[e]) as i:
                    u = first[e] + i
                    for f in range(FC - 1):
                        act.wait_ge(h_made, u * FC + f + 1)
                        nc.scalar.activation(hid[:, f, :], h_psum[:, f, 0:SLOTS], ACT.Relu,
                                             bias=b1c[:, FC * e + f:FC * e + f + 1]).then_inc(relu_act, 1)
                    split_high(u + 3)

            def norm(b, parity):
                act.wait_ge(shift_done, b + 1)
                for j in range(TILES):
                    ins = nc.scalar.activation(normed[:, parity, j, :], z[:, parity, j, :], ACT.Identity,
                                               bias=shift3[:, parity, j:j + 1], scale=rstd3[:, parity, j:j + 1])
                ins.then_inc(n_done, 1)

            with act.Fori(0, B // 2) as pair:
                for parity in range(2):
                    norm(pair * 2 + parity, parity)

        @block.vector
        def _(dve):
            nc.vector.memset(z1[:, 0, 0:1], 0.0).then_inc(y_summed, HALVES)
            nc.vector.memset(z1[:, 0, 1:2], 0.0).then_inc(goals_taken, 1)
            nc.vector.memset(z1[:, 0, 2:3], 0.0).then_inc(lot_turned, 1)
            turns, first = counts_of("vector", dve)

            def split_low(count):
                dve.wait_ge(xh_done, count)
                nc.vector.tensor_tensor(xl[:], x_psum[:, 0, 0:SLOTS], xh[:].bitcast(F32), ALU.subtract)\
                    .then_inc(xl_done, 1)

            def take_goals(v):
                dve.wait_ge(lot_loaded, v * 16 + 16)
                nc.vector.tensor_copy(goals[:, ds(v & (GOALS - 1), 1)],
                                      lot[:, :, D:D + 2].bitcast(U32).unsqueeze(1)).then_inc(goals_taken, 1)

            take_goals(0)
            split_low(1)
            for e in range(E):
                if e == 0:
                    dve.wait_ge(b2_loaded, 16 * 2)
                with dve.Fori(0, turns[e]) as i:
                    u = first[e] + i
                    f = FC - 1
                    dve.wait_ge(h_made, u * FC + FC)
                    nc.vector.tensor_scalar(hid[:, f, :], h_psum[:, f, 0:SLOTS],
                                            b1c[:, FC * e + f:FC * e + f + 1], 0.0, ALU.add, ALU.max)\
                        .then_inc(relu_dve, 1)
                    take_goals(u + 1)
                    split_low(u + 2)
                    for h in range(HALVES):
                        dve.wait_ge(y_made, u * HALVES + h + 1)
                        nc.vector.tensor_tensor(ysum[:, h, :], y_psum[:, h, 0:D], b2b[:, e, :], ALU.add)\
                            .then_inc(y_summed, 1)
                        dve.wait_ge(rows_stored[h], stored_count(u))
                        dve.wait_ge(y_summed, u * HALVES + HALVES + h + 1)
                        nc.vector.tensor_scalar(res[:, h, :], ysum[:, h, :],
                                                goals[:, u & (GOALS - 1), h, 1:2].bitcast(F32), None,
                                                ALU.mult).then_inc(y_done, 1)


            def scale(b, parity):
                if not isinstance(b, int) or b > 1:
                    dve.wait_ge(fin_done, b - 1)
                dve.wait_ge(n_done, b + 1)
                nc.vector.tensor_tensor(scaled[:, parity], normed[:, parity],
                                        gammab[:].unsqueeze(1).to_broadcast([P, TILES, D]), ALU.mult).then_inc(g_done, 1)

            def combine(b, parity, fetched):
                dve.wait_ge(got_in[parity], fetched * 32)
                at = tiles(b)
                nc.vector.tensor_tensor(z1[:], got[:, 0, at, :], kept.xn2[:, at, :], ALU.add).then_inc(z1_done, 1)
                dve.wait_ge(z1_done, b + 1)
                if not isinstance(b, int) or b > 1:
                    dve.wait_ge(n_done, b - 1)
                nc.vector.tensor_tensor(z[:, parity], z1[:], got[:, 1, at, :], ALU.add).then_inc(z_done, 1)
                dve.wait_ge(z_done, b + 1)
                for j in range(TILES):
                    ins = nc.vector.bn_stats(stats3[:, parity, j, :], z[:, parity, j, :])
                ins.then_inc(s3_done, 1)
                dve.wait_ge(s3_done, b + 1)
                if not isinstance(b, int) or b > 1:
                    scale(b - 2, parity)
                for j in range(TILES):
                    ins = nc.vector.bn_aggr(moments3[:, parity, j, :], stats3[:, parity, j, :])
                ins.then_inc(m3_done, 1)

            combine(0, 0, 1)
            combine(1, 1, 1)
            combine(2, 0, 2)
            combine(3, 1, 2)
            with dve.Fori(2, B // 2) as pair:
                for parity in range(2):
                    combine(pair * 2 + parity, parity, pair + 1)
            scale(B - 2, 0)
            scale(B - 1, 1)

        @block.tensor
        def _(pe):
            mm = nc.tensor.matmul
            turns, first = counts_of("tensor", pe)

            def turn_lot(v):
                pe.wait_ge(lot_loaded, v * 16 + 16)
                for h in range(HALVES):
                    ins = nc.tensor.transpose(x_psum[:, 0, P * h:P * h + P], lot[:, h, 0:D], ident[:])
                ins.then_inc(lot_turned, 1)

            turn_lot(0)
            for e in range(E):
                with pe.Fori(0, turns[e]) as i:
                    u = first[e] + i
                    pe.wait_ge(xh_done, u + 1)
                    pe.wait_ge(xl_done, u + 1)
                    for f in range(FC):
                        k = FC * e + f
                        dst = h_psum[:, f, 0:SLOTS]
                        mm(dst, w1h[:, k, :], xh[:], start=True, stop=False)
                        mm(dst, w1h[:, k, :], xl[:], start=False, stop=False)
                        mm(dst, w1l[:, k, :], xh[:], start=False, stop=True).then_inc(h_made, 1)
                    turn_lot(u + 1)
                    for h in range(HALVES):
                        pe.wait_ge(y_summed, u * HALVES + h + 1)
                        for f in range(FC):
                            if h == 0 and f < FC - 1:
                                pe.wait_ge(relu_act, u * (FC - 1) + f + 1)
                            elif h == 0:
                                pe.wait_ge(relu_dve, u + 1)
                            ins = mm(y_psum[:, h, 0:D], hid[:, f, P * h:P * h + P], w2t[:, FC * e + f, :],
                                     start=(f == 0), stop=(f == FC - 1))
                        ins.then_inc(y_made, 1)


_INS = ["L0_attn_x", "L0_attn_Wq", "L0_attn_bq", "L0_attn_Wk", "L0_attn_bk", "L0_attn_Wv", "L0_attn_bv",
        "L0_attn_Wo", "L0_attn_bo", "L0_ffn_Wr", "L0_ffn_br", "L0_ffn_W1", "L0_ffn_b1", "L0_ffn_W2",
        "L0_ffn_b2", "L0_ffn_gamma", "L0_ffn_beta"]


def kernel(**inputs):
    import numpy as _np
    import concourse.bacc as _bacc
    from concourse import mybir as _mybir
    from concourse.bass_utils import run_bass_kernel_spmd as _run

    nc = _bacc.Bacc("TRN2", target_bir_lowering=False, num_devices=1)
    arrays, args = {}, []
    for name in _INS:
        a = _np.ascontiguousarray(inputs[name])
        arrays[f"in_{name}_dram"] = a
        args.append(nc.dram_tensor(f"in_{name}_dram", a.shape, _mybir.dt.from_np(a.dtype), kind="ExternalInput").ap())
    args.append(nc.dram_tensor("out_0_dram", (B, S, D), _mybir.dt.float32, kind="ExternalOutput").ap())
    layer(nc, *args)
    r = _run(nc, [arrays], core_ids=[0])
    return r.results[0]["out_0_dram"]
```
